# Optimizing a Trainium2 kernel written in Bass

```python
import numpy as np
import jax
import jax.numpy as jnp

def _softmax(x, axis=-1):
    return jax.nn.softmax(x, axis=axis)

def _gelu(x):
    return jax.nn.gelu(x, approximate=True)

def _silu(x):
    return jax.nn.silu(x)

def _sigmoid(x):
    return jax.nn.sigmoid(x)

def _layernorm(x, axis=-1, eps=1e-05):
    m = jnp.mean(x, axis=axis, keepdims=True)
    v = jnp.var(x, axis=axis, keepdims=True)
    return (x - m) / jnp.sqrt(v + eps)

def _scatter_add(tgt, idx, src, axis=0):
    return tgt.at[idx].add(src)

def _segment_sum(src, seg, n):
    return jax.ops.segment_sum(src, seg, n)
kernel_name = 'mk_conv_preact_d2_conv_nchw128_r4_5c31e9'

def setup_inputs(seed: int=0):
    np.random.seed(seed)
    _w = jnp.asarray

    def _rec_inputs():
        import jax
        import jax.numpy as jnp
        _gk = jax.random.key(seed)
        x = -0.000125 + 0.9999 * jax.random.normal(jax.random.fold_in(_gk, 1), (4, 32, 64, 64), jnp.float32)
        return x
    x = _rec_inputs()

    def _L0_conv_setup():
        import jax, jax.numpy as jnp
        import numpy as np
        EPS_BR = 0.001
        EPS_ATT = 1e-05

        def _conv(x, w, b=None, pad=0):
            y = jax.lax.conv_general_dilated(x, w, window_strides=(1, 1), padding=((pad, pad), (pad, pad)), dimension_numbers=('NCHW', 'OIHW', 'NCHW'))
            if b is not None:
                y = y + b[None, :, None, None]
            return y

        def _bn(x, gamma, beta, mean, var, eps):
            scale = gamma / jnp.sqrt(var + eps)
            return (x - mean[None, :, None, None]) * scale[None, :, None, None] + beta[None, :, None, None]

        def _position_info(B, H, W, dtype):
            i = jnp.arange(H, dtype=dtype)
            j = jnp.arange(W, dtype=dtype)
            gh = jnp.abs(i - H // 2 + (0.5 if H % 2 == 0 else 0.0)) / float(H // 2)
            gw = jnp.abs(j - W // 2 + (0.5 if W % 2 == 0 else 0.0)) / float(W // 2)
            GH = jnp.broadcast_to(gh[:, None], (H, W))
            GW = jnp.broadcast_to(gw[None, :], (H, W))
            pr = jnp.sqrt(GH ** 2 + GW ** 2)
            k = 2.0 / (pr.max() - pr.min())
            pr = k * pr + (1.0 - pr.max() * k)
            bc = lambda a: jnp.broadcast_to(a[None, None], (B, 1, H, W))
            return (bc(GH), bc(GW), bc(pr))
        key = jax.random.key(seed)
        ks = jax.random.split(key, 16)
        B, Cin, Cout, H, W = (4, 32, 32, 64, 64)
        br = Cout // 2
        s = 0.05
        d = {'x': jax.random.normal(ks[0], (B, Cin, H, W), jnp.float32), 'conv_a_w': jax.random.normal(ks[1], (br, Cin, 3, 3), jnp.float32) * s, 'conv_a_b': jax.random.normal(ks[2], (br,), jnp.float32) * s, 'conv_b_w': jax.random.normal(ks[3], (br, Cin, 3, 3), jnp.float32) * s, 'conv_b_b': jax.random.normal(ks[4], (br,), jnp.float32) * s, 'bn_a_gamma': jnp.ones((br,), jnp.float32), 'bn_a_beta': jnp.zeros((br,), jnp.float32), 'bn_a_mean': jax.random.normal(ks[5], (br,), jnp.float32) * s, 'bn_a_var': jax.random.uniform(ks[6], (br,), jnp.float32, 0.5, 1.5), 'bn_b_gamma': jnp.ones((br,), jnp.float32), 'bn_b_beta': jnp.zeros((br,), jnp.float32), 'bn_b_mean': jax.random.normal(ks[7], (br,), jnp.float32) * s, 'bn_b_var': jax.random.uniform(ks[8], (br,), jnp.float32, 0.5, 1.5), 'att_a_w': jax.random.normal(ks[9], (1, br + 2, 1, 1), jnp.float32) * s, 'att_a_b': jnp.zeros((1,), jnp.float32), 'att_b_w': jax.random.normal(ks[10], (1, br + 2, 1, 1), jnp.float32) * s, 'att_b_b': jnp.zeros((1,), jnp.float32), 'att_bn_a_gamma': jnp.ones((1,), jnp.float32), 'att_bn_a_beta': jnp.zeros((1,), jnp.float32), 'att_bn_a_mean': jnp.zeros((1,), jnp.float32), 'att_bn_a_var': jnp.ones((1,), jnp.float32), 'att_bn_b_gamma': jnp.ones((1,), jnp.float32), 'att_bn_b_beta': jnp.zeros((1,), jnp.float32), 'att_bn_b_mean': jnp.zeros((1,), jnp.float32), 'att_bn_b_var': jnp.ones((1,), jnp.float32), 'attn_a_w': jax.random.normal(ks[11], (1, 4, 3, 3), jnp.float32) * s, 'attn_b_w': jax.random.normal(ks[12], (1, 4, 3, 3), jnp.float32) * s, 'scale1': jnp.asarray(1.0, jnp.float32), 'scale2': jnp.asarray(1.0, jnp.float32)}
        d['attn_a_w'] = d['attn_a_w'].at[:, 3:].set(jnp.abs(d['attn_a_w'][:, 3:]))
        d['attn_b_w'] = d['attn_b_w'].at[:, 3:].set(jnp.abs(d['attn_b_w'][:, 3:]))
        return d
    _L0_conv_all = _L0_conv_setup()
    _L0_conv_in = {k: v for k, v in _L0_conv_all.items() if k in ('conv_a_w', 'conv_a_b', 'conv_b_w', 'conv_b_b', 'bn_a_gamma', 'bn_a_beta', 'bn_a_mean', 'bn_a_var', 'bn_b_gamma', 'bn_b_beta', 'bn_b_mean', 'bn_b_var', 'att_a_w', 'att_a_b', 'att_b_w', 'att_b_b', 'att_bn_a_gamma', 'att_bn_a_beta', 'att_bn_a_mean', 'att_bn_a_var', 'att_bn_b_gamma', 'att_bn_b_beta', 'att_bn_b_mean', 'att_bn_b_var', 'attn_a_w', 'attn_b_w', 'scale1', 'scale2')}
    del _L0_conv_all

    def _L1_conv_setup():
        import jax, jax.numpy as jnp
        import numpy as np
        N, C_IN, C_OUT, K = (4, 32, 32, 3)
        H, W = (24, 24)
        BN_EPS = 1e-05

        def _conv3x3(x, w, b):
            y = jax.lax.conv_general_dilated(x, w, window_strides=(1, 1), padding=((1, 1), (1, 1)), dimension_numbers=('NCHW', 'OIHW', 'NCHW'))
            return y + b[None, :, None, None]

        def _bilinear_gather(img, y, x):
            Hc, Wc = (img.shape[1], img.shape[2])
            y0 = jnp.floor(y)
            x0 = jnp.floor(x)
            y1 = y0 + 1.0
            x1 = x0 + 1.0
            wy1 = y - y0
            wy0 = 1.0 - wy1
            wx1 = x - x0
            wx0 = 1.0 - wx1

            def corner(yc, xc, wgt):
                valid = (yc >= 0) & (yc <= Hc - 1) & (xc >= 0) & (xc <= Wc - 1)
                yi = jnp.clip(yc, 0, Hc - 1).astype(jnp.int32)
                xi = jnp.clip(xc, 0, Wc - 1).astype(jnp.int32)
                v = img[:, yi, xi]
                return v * (wgt * valid.astype(img.dtype))[None, :]
            return corner(y0, x0, wy0 * wx0) + corner(y0, x1, wy0 * wx1) + corner(y1, x0, wy1 * wx0) + corner(y1, x1, wy1 * wx1)

        def _dcnv2(x, offset_w, offset_b, mod_w, mod_b, weight, bias, gamma, beta):
            Nb, C, Hh, Ww = x.shape
            KK = K * K
            offs = _conv3x3(x, offset_w, offset_b).reshape(Nb, KK, 2, Hh, Ww)
            off_y, off_x = (offs[:, :, 0], offs[:, :, 1])
            mask = 2.0 * jax.nn.sigmoid(_conv3x3(x, mod_w, mod_b))
            kyy, kxx = jnp.meshgrid(jnp.arange(K) - 1, jnp.arange(K) - 1, indexing='ij')
            kyy = kyy.reshape(KK).astype(x.dtype)
            kxx = kxx.reshape(KK).astype(x.dtype)
            hy = jnp.arange(Hh, dtype=x.dtype)
            wx = jnp.arange(Ww, dtype=x.dtype)
            sy = off_y + hy[None, None, :, None] + kyy[None, :, None, None]
            sx = off_x + wx[None, None, None, :] + kxx[None, :, None, None]
            P = KK * Hh * Ww

            def per_img(img, yy, xx):
                return _bilinear_gather(img, yy.reshape(P), xx.reshape(P))
            sampled = jax.vmap(per_img)(x, sy, sx).reshape(Nb, C, KK, Hh, Ww)
            sampled = sampled * mask[:, None]
            w = weight.reshape(C_OUT, C, KK)
            out = jnp.einsum('nckhw,ock->nohw', sampled, w) + bias[None, :, None, None]
            mean = out.mean(axis=(0, 2, 3), keepdims=True)
            var = ((out - mean) ** 2).mean(axis=(0, 2, 3), keepdims=True)
            out = (out - mean) * jax.lax.rsqrt(var + BN_EPS)
            out = out * gamma[None, :, None, None] + beta[None, :, None, None]
            return jax.nn.relu(out)
        key = jax.random.key(seed)
        ks = jax.random.split(key, 6)
        x = jax.random.normal(ks[0], (N, C_IN, H, W), jnp.float32)
        offset_w = jax.random.normal(ks[1], (2 * K * K, C_IN, K, K), jnp.float32) * 0.01
        offset_b = jnp.zeros((2 * K * K,), jnp.float32)
        mod_w = jax.random.normal(ks[2], (K * K, C_IN, K, K), jnp.float32) * 0.01
        mod_b = jnp.zeros((K * K,), jnp.float32)
        fan_in = C_IN * K * K
        weight = jax.random.normal(ks[3], (C_OUT, C_IN, K, K), jnp.float32) / np.sqrt(fan_in).astype(np.float32)
        bias = jax.random.normal(ks[4], (C_OUT,), jnp.float32) * 0.01
        gamma = jnp.ones((C_OUT,), jnp.float32)
        beta = jnp.zeros((C_OUT,), jnp.float32)
        return dict(x=x, offset_w=offset_w, offset_b=offset_b, mod_w=mod_w, mod_b=mod_b, weight=weight, bias=bias, gamma=gamma, beta=beta)
    _L1_conv_all = _L1_conv_setup()
    _L1_conv_in = {k: v for k, v in _L1_conv_all.items() if k in ('offset_w', 'offset_b', 'mod_w', 'mod_b', 'weight', 'bias', 'gamma', 'beta')}
    del _L1_conv_all
    return {'x': x, 'L0_conv_conv_a_w': _L0_conv_in['conv_a_w'], 'L0_conv_conv_a_b': _L0_conv_in['conv_a_b'], 'L0_conv_conv_b_w': _L0_conv_in['conv_b_w'], 'L0_conv_conv_b_b': _L0_conv_in['conv_b_b'], 'L0_conv_bn_a_gamma': _L0_conv_in['bn_a_gamma'], 'L0_conv_bn_a_beta': _L0_conv_in['bn_a_beta'], 'L0_conv_bn_a_mean': _L0_conv_in['bn_a_mean'], 'L0_conv_bn_a_var': _L0_conv_in['bn_a_var'], 'L0_conv_bn_b_gamma': _L0_conv_in['bn_b_gamma'], 'L0_conv_bn_b_beta': _L0_conv_in['bn_b_beta'], 'L0_conv_bn_b_mean': _L0_conv_in['bn_b_mean'], 'L0_conv_bn_b_var': _L0_conv_in['bn_b_var'], 'L0_conv_att_a_w': _L0_conv_in['att_a_w'], 'L0_conv_att_a_b': _L0_conv_in['att_a_b'], 'L0_conv_att_b_w': _L0_conv_in['att_b_w'], 'L0_conv_att_b_b': _L0_conv_in['att_b_b'], 'L0_conv_att_bn_a_gamma': _L0_conv_in['att_bn_a_gamma'], 'L0_conv_att_bn_a_beta': _L0_conv_in['att_bn_a_beta'], 'L0_conv_att_bn_a_mean': _L0_conv_in['att_bn_a_mean'], 'L0_conv_att_bn_a_var': _L0_conv_in['att_bn_a_var'], 'L0_conv_att_bn_b_gamma': _L0_conv_in['att_bn_b_gamma'], 'L0_conv_att_bn_b_beta': _L0_conv_in['att_bn_b_beta'], 'L0_conv_att_bn_b_mean': _L0_conv_in['att_bn_b_mean'], 'L0_conv_att_bn_b_var': _L0_conv_in['att_bn_b_var'], 'L0_conv_attn_a_w': _L0_conv_in['attn_a_w'], 'L0_conv_attn_b_w': _L0_conv_in['attn_b_w'], 'L0_conv_scale1': _L0_conv_in['scale1'], 'L0_conv_scale2': _L0_conv_in['scale2'], 'L1_conv_offset_w': _L1_conv_in['offset_w'], 'L1_conv_offset_b': _L1_conv_in['offset_b'], 'L1_conv_mod_w': _L1_conv_in['mod_w'], 'L1_conv_mod_b': _L1_conv_in['mod_b'], 'L1_conv_weight': _L1_conv_in['weight'], 'L1_conv_bias': _L1_conv_in['bias'], 'L1_conv_gamma': _L1_conv_in['gamma'], 'L1_conv_beta': _L1_conv_in['beta']}

def reference(x, L0_conv_conv_a_w, L0_conv_conv_a_b, L0_conv_conv_b_w, L0_conv_conv_b_b, L0_conv_bn_a_gamma, L0_conv_bn_a_beta, L0_conv_bn_a_mean, L0_conv_bn_a_var, L0_conv_bn_b_gamma, L0_conv_bn_b_beta, L0_conv_bn_b_mean, L0_conv_bn_b_var, L0_conv_att_a_w, L0_conv_att_a_b, L0_conv_att_b_w, L0_conv_att_b_b, L0_conv_att_bn_a_gamma, L0_conv_att_bn_a_beta, L0_conv_att_bn_a_mean, L0_conv_att_bn_a_var, L0_conv_att_bn_b_gamma, L0_conv_att_bn_b_beta, L0_conv_att_bn_b_mean, L0_conv_att_bn_b_var, L0_conv_attn_a_w, L0_conv_attn_b_w, L0_conv_scale1, L0_conv_scale2, L1_conv_offset_w, L1_conv_offset_b, L1_conv_mod_w, L1_conv_mod_b, L1_conv_weight, L1_conv_bias, L1_conv_gamma, L1_conv_beta):
    import jax
    import jax.numpy as jnp

    def _L0_conv_ref(x, conv_a_w, conv_a_b, conv_b_w, conv_b_b, bn_a_gamma, bn_a_beta, bn_a_mean, bn_a_var, bn_b_gamma, bn_b_beta, bn_b_mean, bn_b_var, att_a_w, att_a_b, att_b_w, att_b_b, att_bn_a_gamma, att_bn_a_beta, att_bn_a_mean, att_bn_a_var, att_bn_b_gamma, att_bn_b_beta, att_bn_b_mean, att_bn_b_var, attn_a_w, attn_b_w, scale1, scale2):
        import jax, jax.numpy as jnp
        import numpy as np
        EPS_BR = 0.001
        EPS_ATT = 1e-05

        def _conv(x, w, b=None, pad=0):
            y = jax.lax.conv_general_dilated(x, w, window_strides=(1, 1), padding=((pad, pad), (pad, pad)), dimension_numbers=('NCHW', 'OIHW', 'NCHW'))
            if b is not None:
                y = y + b[None, :, None, None]
            return y

        def _bn(x, gamma, beta, mean, var, eps):
            scale = gamma / jnp.sqrt(var + eps)
            return (x - mean[None, :, None, None]) * scale[None, :, None, None] + beta[None, :, None, None]

        def _position_info(B, H, W, dtype):
            i = jnp.arange(H, dtype=dtype)
            j = jnp.arange(W, dtype=dtype)
            gh = jnp.abs(i - H // 2 + (0.5 if H % 2 == 0 else 0.0)) / float(H // 2)
            gw = jnp.abs(j - W // 2 + (0.5 if W % 2 == 0 else 0.0)) / float(W // 2)
            GH = jnp.broadcast_to(gh[:, None], (H, W))
            GW = jnp.broadcast_to(gw[None, :], (H, W))
            pr = jnp.sqrt(GH ** 2 + GW ** 2)
            k = 2.0 / (pr.max() - pr.min())
            pr = k * pr + (1.0 - pr.max() * k)
            bc = lambda a: jnp.broadcast_to(a[None, None], (B, 1, H, W))
            return (bc(GH), bc(GW), bc(pr))
        fa = _bn(_conv(x, conv_a_w, conv_a_b, pad=1), bn_a_gamma, bn_a_beta, bn_a_mean, bn_a_var, EPS_BR)
        fb = _bn(_conv(x, conv_b_w, conv_b_b, pad=1), bn_b_gamma, bn_b_beta, bn_b_mean, bn_b_var, EPS_BR)
        B, _, H, W = fa.shape
        gh, gw, pr = _position_info(B, H, W, fa.dtype)
        att_a = _bn(_conv(jnp.concatenate([fa, gh, gw], axis=1), att_a_w, att_a_b), att_bn_a_gamma, att_bn_a_beta, att_bn_a_mean, att_bn_a_var, EPS_ATT)
        att_b = _bn(_conv(jnp.concatenate([fb, gh, gw], axis=1), att_b_w, att_b_b), att_bn_b_gamma, att_bn_b_beta, att_bn_b_mean, att_bn_b_var, EPS_ATT)
        map_a = jax.nn.sigmoid(_conv(jnp.concatenate([att_a, gh, gw, pr], axis=1), attn_a_w, pad=1))
        map_b = jax.nn.sigmoid(_conv(jnp.concatenate([att_b, gh, gw, pr], axis=1), attn_b_w, pad=1))
        out = jnp.concatenate([fa * (map_a * scale1), fb * (map_b * scale2)], axis=1)
        return out

    def _L1_conv_ref(x, offset_w, offset_b, mod_w, mod_b, weight, bias, gamma, beta):
        import jax, jax.numpy as jnp
        import numpy as np
        N, C_IN, C_OUT, K = (4, 32, 32, 3)
        H, W = (24, 24)
        BN_EPS = 1e-05

        def _conv3x3(x, w, b):
            y = jax.lax.conv_general_dilated(x, w, window_strides=(1, 1), padding=((1, 1), (1, 1)), dimension_numbers=('NCHW', 'OIHW', 'NCHW'))
            return y + b[None, :, None, None]

        def _bilinear_gather(img, y, x):
            Hc, Wc = (img.shape[1], img.shape[2])
            y0 = jnp.floor(y)
            x0 = jnp.floor(x)
            y1 = y0 + 1.0
            x1 = x0 + 1.0
            wy1 = y - y0
            wy0 = 1.0 - wy1
            wx1 = x - x0
            wx0 = 1.0 - wx1

            def corner(yc, xc, wgt):
                valid = (yc >= 0) & (yc <= Hc - 1) & (xc >= 0) & (xc <= Wc - 1)
                yi = jnp.clip(yc, 0, Hc - 1).astype(jnp.int32)
                xi = jnp.clip(xc, 0, Wc - 1).astype(jnp.int32)
                v = img[:, yi, xi]
                return v * (wgt * valid.astype(img.dtype))[None, :]
            return corner(y0, x0, wy0 * wx0) + corner(y0, x1, wy0 * wx1) + corner(y1, x0, wy1 * wx0) + corner(y1, x1, wy1 * wx1)

        def _dcnv2(x, offset_w, offset_b, mod_w, mod_b, weight, bias, gamma, beta):
            Nb, C, Hh, Ww = x.shape
            KK = K * K
            offs = _conv3x3(x, offset_w, offset_b).reshape(Nb, KK, 2, Hh, Ww)
            off_y, off_x = (offs[:, :, 0], offs[:, :, 1])
            mask = 2.0 * jax.nn.sigmoid(_conv3x3(x, mod_w, mod_b))
            kyy, kxx = jnp.meshgrid(jnp.arange(K) - 1, jnp.arange(K) - 1, indexing='ij')
            kyy = kyy.reshape(KK).astype(x.dtype)
            kxx = kxx.reshape(KK).astype(x.dtype)
            hy = jnp.arange(Hh, dtype=x.dtype)
            wx = jnp.arange(Ww, dtype=x.dtype)
            sy = off_y + hy[None, None, :, None] + kyy[None, :, None, None]
            sx = off_x + wx[None, None, None, :] + kxx[None, :, None, None]
            P = KK * Hh * Ww

            def per_img(img, yy, xx):
                return _bilinear_gather(img, yy.reshape(P), xx.reshape(P))
            sampled = jax.vmap(per_img)(x, sy, sx).reshape(Nb, C, KK, Hh, Ww)
            sampled = sampled * mask[:, None]
            w = weight.reshape(C_OUT, C, KK)
            out = jnp.einsum('nckhw,ock->nohw', sampled, w) + bias[None, :, None, None]
            mean = out.mean(axis=(0, 2, 3), keepdims=True)
            var = ((out - mean) ** 2).mean(axis=(0, 2, 3), keepdims=True)
            out = (out - mean) * jax.lax.rsqrt(var + BN_EPS)
            out = out * gamma[None, :, None, None] + beta[None, :, None, None]
            return jax.nn.relu(out)
        return _dcnv2(x, offset_w, offset_b, mod_w, mod_b, weight, bias, gamma, beta)

    def _gn(v, G=32, eps=1e-05):
        B_, C_, H_, W_ = v.shape
        g = v.reshape(B_, G, C_ // G, H_, W_)
        m = jnp.mean(g, axis=(2, 3, 4), keepdims=True)
        s = jnp.var(g, axis=(2, 3, 4), keepdims=True)
        return ((g - m) / jnp.sqrt(s + eps)).reshape(v.shape)

    def _ln_c(v, eps=1e-06):
        m = jnp.mean(v, axis=1, keepdims=True)
        s = jnp.var(v, axis=1, keepdims=True)
        return (v - m) / jnp.sqrt(s + eps)

    def _ln_t(v, eps=1e-05):
        m = jnp.mean(v, axis=-1, keepdims=True)
        s = jnp.var(v, axis=-1, keepdims=True)
        return (v - m) / jnp.sqrt(s + eps)

    def _to_tokens(v):
        B_, C_, H_, W_ = v.shape
        return v.reshape(B_, C_, H_ * W_).transpose(0, 2, 1)

    def _from_tokens(t, like):
        B_, C_, H_, W_ = like.shape
        return t.transpose(0, 2, 1).reshape(B_, C_, H_, W_)
    x = x + _L0_conv_ref(_gn(x), L0_conv_conv_a_w, L0_conv_conv_a_b, L0_conv_conv_b_w, L0_conv_conv_b_b, L0_conv_bn_a_gamma, L0_conv_bn_a_beta, L0_conv_bn_a_mean, L0_conv_bn_a_var, L0_conv_bn_b_gamma, L0_conv_bn_b_beta, L0_conv_bn_b_mean, L0_conv_bn_b_var, L0_conv_att_a_w, L0_conv_att_a_b, L0_conv_att_b_w, L0_conv_att_b_b, L0_conv_att_bn_a_gamma, L0_conv_att_bn_a_beta, L0_conv_att_bn_a_mean, L0_conv_att_bn_a_var, L0_conv_att_bn_b_gamma, L0_conv_att_bn_b_beta, L0_conv_att_bn_b_mean, L0_conv_att_bn_b_var, L0_conv_attn_a_w, L0_conv_attn_b_w, L0_conv_scale1, L0_conv_scale2)
    x = x + _L1_conv_ref(_gn(x), L1_conv_offset_w, L1_conv_offset_b, L1_conv_mod_w, L1_conv_mod_b, L1_conv_weight, L1_conv_bias, L1_conv_gamma, L1_conv_beta)
    return x

_drawn_inputs = setup_inputs


def setup_inputs(seed=0):
    import zlib

    import numpy as np

    out = dict(_drawn_inputs(seed))
    spreads = {'L0_conv_bn_a_gamma': (1.0, 0.2),
     'L0_conv_bn_a_beta': (0.0, 0.316),
     'L0_conv_bn_b_gamma': (1.0, 0.2),
     'L0_conv_bn_b_beta': (0.0, 0.271),
     'L1_conv_offset_b': (0.0, 0.1),
     'L1_conv_mod_b': (0.0, 0.8),
     'L1_conv_gamma': (1.0, 0.2),
     'L1_conv_beta': (0.0, 0.1)}
    factors = {'L0_conv_conv_a_b': 4.211,
     'L0_conv_conv_b_b': 4.248,
     'L0_conv_bn_a_mean': 5.735,
     'L0_conv_bn_b_mean': 5.357,
     'L0_conv_att_a_w': 8.0,
     'L0_conv_att_b_w': 8.0,
     'L1_conv_bias': 8.0}
    for name, (base, spread) in spreads.items():
        noise = np.random.default_rng([zlib.crc32(name.encode()), seed]).standard_normal(out[name].shape)
        drawn = base * np.exp(spread * noise) if base else spread * noise
        out[name] = jnp.asarray(drawn.astype(out[name].dtype))
    for name, factor in factors.items():
        out[name] = (out[name] * factor).astype(out[name].dtype)
    return out
```

```python
import concourse.bass as bass
from concourse import mybir
from contextlib import ExitStack
import numpy as np

B, C, H, W = 4, 32, 64, 64
NPIX = H * W
KK = 9
BR = C // 2
P128 = B * C
PAD_T = 2
XR, XC = H + 6, W + 2
AR = H + 2
CH_ROWS = 8
NCH = H // CH_ROWS
HH = H // 2
NT = B * HH
NOFF = 27
NCOL = B * NOFF
ATT_ROWS = KK * B * 2
POS_ROWS = KK * 4
MAP_ROWS = ATT_ROWS + POS_ROWS
IMLEN = H * AR
NPART = 3
SELK = NPART * B * 2 + 2
KW = KK * C
G3 = 3 * C
GW = KK * G3
ZLEAD = 6
ZSLOTS = HH + ZLEAD
BR_EPS, ATT_EPS, GN_EPS, BN_EPS = 1e-3, 1e-5, 1e-5, 1e-5
BANK = 512
CREDIT = 2

V_CB, V_GAMMA, V_BETA, V_MEAN, V_VAR, V_ATTW, V_SCALE, V_DBIAS, V_DGAMMA, V_DBETA = range(10)
A_WGH, A_WGW, A_B, A_GAMMA, A_BETA, A_MEAN, A_VAR = range(7)


def conv_deform_kernel(nc, d, out):
    f32 = mybir.dt.float32
    bf16 = mybir.dt.bfloat16
    ALU = mybir.AluOpType
    ACT = mybir.ActivationFunctionType
    AX = mybir.AxisListType
    ds = bass.ds

    ctx = ExitStack()
    with ctx:
        def sb(name, shape, dt=f32):
            return ctx.enter_context(nc.sbuf_tensor(name, shape, dt))

        def sem(name):
            return ctx.enter_context(nc.semaphore(name))

        x_sb = sb("x_sb", [P128, NPIX])
        xpad = sb("xpad", [P128, XR, XC])
        w0 = sb("w0", [P128, KK, P128])
        woff = sb("woff", [P128, KK, NCOL])
        wz = sb("wz", [P128, B, KW])
        vec = sb("vec", [P128, 10])
        attp = sb("attp", [MAP_ROWS, 7, 2])
        attt = sb("attt", [MAP_ROWS, 2, 2])
        rowm = sb("rowm", [MAP_ROWS, 5])
        blkm = sb("blkm", [MAP_ROWS, 2, P128])
        mapw = sb("mapw", [MAP_ROWS, P128])
        attm = sb("attm", [P128, B * 2])
        attw = sb("attw", [P128, B * 2])
        offb = sb("offb", [P128, NCOL])
        rbias = sb("rbias", [P128, 3])
        bstats = sb("bstats", [P128, 2 * NCH, 6])
        avg4 = sb("avg4", [P128, P128])
        identf = sb("identf", [P128, P128])
        identh = sb("identh", [P128, P128], bf16)
        sel = sb("sel", [SELK, B + 1, P128], bf16)
        small = sb("small", [P128, 64])
        stats = sb("stats", [P128, NCH, 6])
        offs = sb("offs", [P128, HH, NCOL])
        hy = sb("hy", [P128, 3, HH * B * KK])
        stage = sb("stage", [P128, 4, 3, 2 * W])
        dist = sb("dist", [P128, 2, KK * W])
        hx = sb("hx", [P128, 2, KK, 2 * W])
        prod = sb("prod", [P128, 2, GW])
        reach = sb("reach", [P128, HH * B])
        reach_c = sb("reach_c", [P128, 2])
        reach_i = sb("reach_i", [1, HH * B], mybir.dt.int32)
        reach_b = sb("reach_b", [1, B], mybir.dt.int32)
        far_x = sb("far_x", [P128, 3, 2 * W])
        far_z = sb("far_z", [P128, KW])
        far_r = sb("far_r", [P128, 1])
        far_w = sb("far_w", [P128, KK])
        far_u = sb("far_u", [P128, KK])
        far_p = sb("far_p", [P128, KW])
        far_s = sb("far_s", [P128, C])
        zreg = sb("zreg", [P128, ZSLOTS, KW])
        preg = sb("preg", [P128, KK * HH * W], bf16)
        areg = sb("areg", [P128, NPIX])

        z_sb = zreg
        zflat = zreg[:, :, :].rearrange("p a n -> p (a n)")
        attpad = zflat[0:B * 2, 0:AR * AR]
        im2col = zflat[0:MAP_ROWS, AR * AR:AR * AR + IMLEN]
        out_t = zflat[:, 0:NPIX]
        f_sb = preg[:, 0:2 * NPIX].bitcast(f32)
        px = preg[0:SELK, :].rearrange("p (k n) -> p k n", k=KK)
        acc = areg[:, :].rearrange("p (y b o) -> p y b o", y=HH, b=B)
        tpart = areg[:, 0:NPIX // 2].bitcast(bf16)
        parts = areg[:, NPIX // 2:NPIX // 2 + HH * NPART * B * KK // 2].bitcast(bf16)\
            .rearrange("p (y q n) -> p y q n", y=HH, q=NPART)
        sig = dist[:, :, 0:BANK]
        hyt = prod[:, :, :].rearrange("p a n -> p (a n)")[:, 0:HH * B * KK]
        ps = ctx.enter_context(nc.psum_tensor("ps", [P128, 8 * BANK], f32))

        x_loaded = [sem(f"x_loaded{i}") for i in range(4)]
        zeroed = sem("zeroed")
        w0_loaded = sem("w0_loaded")
        params_loaded = sem("params_loaded")
        map_loaded = sem("map_loaded")
        late_loaded = sem("late_loaded")
        vchain = sem("vchain")
        st_ready = sem("st_ready")
        pool_turns = sem("pool_turns")
        root_in = sem("root_in")
        root_done = sem("root_done")
        x1_ready = sem("x1_ready")
        rbias_ready = sem("rbias_ready")
        xpad_zeroed = sem("xpad_zeroed")
        attpad_zeroed = sem("attpad_zeroed")
        norm1 = sem("norm1")
        bn0_ready = sem("bn0_ready")
        attw_ready = sem("attw_ready")
        mapw_ready = sem("mapw_ready")
        conv_ready = sem("conv_ready")
        f_ready = sem("f_ready")
        att_ready = sem("att_ready")
        att_saved = sem("att_saved")
        im2col_ready = sem("im2col_ready")
        map_ready = sem("map_ready")
        sig_ready = sem("sig_ready")
        sig_used = sem("sig_used")
        norm2 = sem("norm2")
        row_staged = sem("row_staged")
        hx_zeroed = sem("hx_zeroed")
        hx_ready = sem("hx_ready")
        off_ready = sem("off_ready")
        off_saved = sem("off_saved")
        parts_ready = sem("parts_ready")
        tp_ready = sem("tp_ready")
        tp_saved = sem("tp_saved")
        px_ready = sem("px_ready")
        mod_ready = sem("mod_ready")
        hya_ready = sem("hya_ready")
        zrow_staged = sem("zrow_staged")
        zrow_made = sem("zrow_made")
        zrow_saved = sem("zrow_saved")
        dist_made = sem("dist_made")
        dist_ready = sem("dist_ready")
        g_ready = sem("g_ready")
        g_used = sem("g_used")
        acc_ready = sem("acc_ready")
        acc_final = sem("acc_final")
        outt_made = sem("outt_made")
        outt_saved = sem("outt_saved")
        bst_ready = sem("bst_ready")
        bmean_ready = sem("bmean_ready")
        bvar_in = sem("bvar_in")
        bvar_ready = sem("bvar_ready")
        bnc_ready = sem("bnc_ready")
        relu_ready = sem("relu_ready")
        res_ready = sem("res_ready")
        stored = sem("stored")
        reach_in = sem("reach_in")
        reach_t = sem("reach_t")
        reach_col = sem("reach_col")
        reach_row = sem("reach_row")
        reach_ready = sem("reach_ready")
        far_staged = sem("far_staged")
        far_zmade = sem("far_zmade")
        far_zsaved = sem("far_zsaved")
        far_made = sem("far_made")
        far_used = sem("far_used")
        far_turns = sem("far_turns")

        offv = offs[:, :, :].rearrange("p y (b j k) -> p y b j k", b=B, j=3)
        oy_v, ox_v, mod_v = (offv[:, :, :, j, :] for j in range(3))

        def per_tile(ap):
            return ap.rearrange("p (y b k) -> p y b k", y=HH, b=B)

        dist_ps = ps[:, 0:KK * W]

        TAPS = (range(0, BANK // G3), range(BANK // G3, KK))

        def g_ps(u, h):
            at = (2 + 2 * u + h) * BANK
            return ps[:, at:at + len(TAPS[h]) * G3].rearrange("p (k r o) -> p k r o", r=3, o=C)

        far_ps = ps[:, 2 * BANK:2 * BANK + KW]

        def z_ps(u):
            return ps[:, (6 + u) * BANK:(6 + u) * BANK + KW]

        def pair(row):
            return xpad[:, ds(row, 2, step=HH), :]

        def col(i, n=P128):
            return small[0:n, i:i + 1]

        MV, RSTD, BS, BB, MV2, RSTD2, MVB, SQ, MEANB, DB, VARB, SC, SH, T0, T1 = \
            0, 2, 3, 4, 5, 7, 8, 10, 11, 12, 13, 14, 15, 16, 17
        ROOT_IN, ROOT_OUT, ROOT_TMP = 40, 44, 48
        NLATE = 2 * B + 5
        block = ctx.enter_context(nc.Block())

        FAR = H + 2

        def far_rows(eng, tile, turn):
            tiles, turns = eng.alloc_register("far_tiles"), eng.alloc_register("far_turn")
            eng.reg_mov(tiles, 0)
            eng.reg_mov(turns, 0)
            with eng.Fori(0, B) as b:
                rb = eng.value_load(reach_b[0:1, ds(b, 1)], min_val=0, max_val=FAR)
                with eng.If(rb >= 1):
                    with eng.Fori(0, HH) as y:
                        rt = eng.value_load(reach_i[0:1, ds(y * B + b, 1)], min_val=0, max_val=FAR)
                        with eng.If(rt >= 1):
                            tile(b, y, eng.snap(tiles, min_val=0, max_val=NT))
                            eng.reg_add(tiles, tiles, 1)
                            with eng.Fori(1, rt + 1) as e:
                                n = eng.snap(turns, min_val=0, max_val=2 * NT * FAR)
                                for i, sign in enumerate((1, -1)):
                                    turn(b, y, e + 1, sign, n + i)
                                eng.reg_add(turns, turns, 2)

        @block.sync
        def _(sync):
            for q in range(4):
                n = NPIX // 4
                sync.dma_start(x_sb[:, q * n:(q + 1) * n], d["x"][:, q * n:(q + 1) * n])\
                    .then_inc(x_loaded[q], 16)
            sync.wait_ge(zeroed, 3)
            for b in range(B):
                s = slice(b * C, (b + 1) * C)
                sync.dma_start(w0[s, :, s], d["w0"]).then_inc(w0_loaded, 16)
            sync.dma_start(im2col[ATT_ROWS:MAP_ROWS, :], d["pos"]).then_inc(im2col_ready, 16)
            for b in range(B):
                s = slice(b * C, (b + 1) * C)
                sync.dma_start(woff[s, :, b * NOFF:(b + 1) * NOFF], d["woff"]).then_inc(late_loaded, 16)
                sync.dma_start(wz[s, b, :], d["wz"]).then_inc(late_loaded, 16)
            sync.dma_start(offb[:, :], d["offb"]).then_inc(late_loaded, 16)
            sync.dma_start(avg4[:, :], d["avg4"]).then_inc(late_loaded, 16)
            sync.dma_start(identf[:, :], d["identf"]).then_inc(late_loaded, 16)
            sync.dma_start(identh[:, :], d["identh"].bitcast(bf16)).then_inc(late_loaded, 16)
            sync.dma_start(sel[:, :, :], d["sel"].bitcast(bf16)).then_inc(late_loaded, 16)
            sync.wait_ge(att_saved, NCH + CREDIT)
            for t in range(KK):
                o = (t // 3) * AR + t % 3
                sync.dma_start(im2col[t * B * 2:(t + 1) * B * 2, 0:IMLEN - 2],
                               attpad[:, o:o + IMLEN - 2]).then_inc(im2col_ready, 16)
            sync.wait_ge(sig_used, NCH + CREDIT)
            sync.dma_start(px[SELK - 2:SELK, :, :], d["prow"].bitcast(bf16)).then_inc(px_ready, 16)
            sync.wait_ge(tp_saved, 4 + CREDIT)
            n = HH * W
            for q in range(NPART * B):
                for g in range(2):
                    sync.dma_start(px[2 * q + g:2 * q + g + 1, :, :],
                                   tpart[q * KK:(q + 1) * KK, g * n:(g + 1) * n])\
                        .then_inc(px_ready, 16)
            for c in range(NCH):
                sync.wait_ge(res_ready, c + 1)
                sync.dma_start(out[:, c * BANK:(c + 1) * BANK], x_sb[:, c * BANK:(c + 1) * BANK])\
                    .then_inc(stored, 16)
            sync.wait_ge(stored, 16 * NCH)

        @block.gpsimd
        def _(pool):
            pool.memset(xpad[:, :, :], 0.0).then_inc(xpad_zeroed, 1)
            pool.memset(w0[:, :, :], 0.0).then_inc(zeroed, 1)
            pool.memset(woff[:, :, :], 0.0).then_inc(zeroed, 1)
            pool.memset(wz[:, :, :], 0.0).then_inc(zeroed, 1)
            pool.memset(attpad, 0.0).then_inc(attpad_zeroed, 1)
            pool.memset(hx[:, :, :, :], 0.0).then_inc(hx_zeroed, 1)
            def stage_row(slot, row):
                for dx in range(3):
                    pool.tensor_copy(stage[:, slot, dx, :].rearrange("p (g x) -> p g x", g=2),
                                     pair(row)[:, :, dx:dx + W]).then_inc(row_staged, 1)

            pool.wait_ge(norm2, 1)
            stage_row(3, PAD_T - 1)
            stage_row(0, PAD_T)
            with pool.Fori(0, HH // 4) as iy:
                y = iy * 4
                for u in range(4):
                    pool.wait_ge(off_ready, y + (u - 1 + CREDIT))
                    pool.sem_inc(pool_turns, 1)
                    stage_row((u + 1) % 4, y + (u + 1 + PAD_T))

            def stage_z(n, u, row):
                pool.wait_ge(zrow_made, n + (CREDIT - 1))
                pool.sem_inc(pool_turns, 1)
                pool.tensor_copy(stage[:, u, 0, :].rearrange("p (g x) -> p g x", g=2),
                                 pair(row)[:, :, 1:1 + W]).then_inc(zrow_staged, 1)

            pool.wait_ge(off_ready, HH + CREDIT)
            with pool.Fori(0, B) as b:
                with pool.Fori(0, ZSLOTS // 2) as iy:
                    for u in range(2):
                        stage_z(b * ZSLOTS + iy * 2 + u, u, iy * 2 + u)

            far_row = pool.alloc_register("far_row")

            def far_stage(b, y, row, sign, n):
                pool.wait_ge(far_zmade, n + CREDIT)
                pool.sem_inc(pool_turns, 1)
                for ky in range(3):
                    for g in range(2):
                        at = y + (g * HH + ky - 1 + PAD_T) + (row if sign > 0 else row * -1)
                        pool.reg_alu(far_row, at + FAR, FAR + PAD_T - 1, ALU.max)
                        pool.reg_alu(far_row, far_row, FAR + PAD_T + H, ALU.min)
                        pool.reg_alu(far_row, far_row, FAR, ALU.subtract)
                        r = pool.snap(far_row, min_val=PAD_T - 1, max_val=PAD_T + H)
                        pool.tensor_copy(far_x[:, ky, g * W:(g + 1) * W],
                                         xpad[:, ds(r, 1), 1:1 + W].rearrange("p a x -> p (a x)"))\
                            .then_inc(far_staged, 1)

            pool.wait_ge(reach_ready, 2)
            far_rows(pool, lambda b, y, n: None, far_stage)

        @block.tensor
        def _(pe):
            pe.wait_ge(norm1, 1)
            pe.wait_ge(w0_loaded, 16 * B)
            pe.wait_ge(attw_ready, 1)

            def att_chunk(c, u):
                pe.wait_ge(f_ready, c + (1 + CREDIT))
                pe.matmul(ps[0:B * 2, (2 + u) * BANK:(3 + u) * BANK], attw[:, :],
                          f_sb[:, ds(c * BANK, BANK)], start=True, stop=True).then_inc(att_ready, 1)

            with pe.Fori(0, NCH // 2) as ic:
                c = ic * 2
                for u in range(2):
                    pe.wait_ge(f_ready, c + CREDIT)
                    for t in range(KK):
                        rows = xpad[:, ds((c + u) * CH_ROWS + (PAD_T - 1 + t // 3), CH_ROWS),
                                    t % 3:t % 3 + W]
                        mm = pe.matmul(ps[:, u * BANK:(u + 1) * BANK], w0[:, t, :], rows,
                                       start=t == 0, stop=t == KK - 1)
                    mm.then_inc(conv_ready, 1)
                for u in range(2):
                    pe.wait_ge(att_saved, c + CREDIT)
                    att_chunk(c + u, u)

            pe.wait_ge(mapw_ready, 1)
            pe.wait_ge(im2col_ready, 16 * (KK + 1))
            with pe.Fori(0, NCH // 2) as ic:
                c = ic * 2
                for u in range(2):
                    pe.wait_ge(sig_ready, c + CREDIT)
                    rows = im2col[:, ds((c + u) * (CH_ROWS * AR), CH_ROWS * AR)]\
                        .rearrange("p (r x) -> p r x", x=AR)[:, :, 0:W]
                    pe.matmul(ps[:, (4 + u) * BANK:(5 + u) * BANK], mapw[:, :], rows,
                              start=True, stop=True).then_inc(map_ready, 1)

            pe.wait_ge(late_loaded, 16 * NLATE)
            with pe.Fori(0, HH // 4) as iy:
                y = iy * 4
                for u in range(4):
                    pe.wait_ge(row_staged, y * 3 + (u + 3) * 3)
                    pe.wait_ge(off_saved, y + (u - 1 + CREDIT))
                    for t in range(KK):
                        mm = pe.matmul(ps[:, (u % 2) * BANK:(u % 2) * BANK + NCOL],
                                       stage[:, (u + t // 3 - 1) % 4, t % 3, :],
                                       woff[:, t, :], start=t == 0, stop=t == KK - 1)
                    mm.then_inc(off_ready, 1)

            pe.wait_ge(parts_ready, 1)
            with pe.Fori(0, HH // 16) as iy:
                y = iy * 16
                for u in range(2):
                    bank = ps[0:NPART * B * KK, (2 + u) * BANK:(3 + u) * BANK].bitcast(bf16)
                    pe.wait_ge(tp_saved, y // 8 + CREDIT)
                    for i in range(8):
                        mm = pe.transpose(bank[:, i * P128:(i + 1) * P128],
                                          parts[:, ds(y + (8 * u + i), 1), :, :]
                                          .rearrange("p y q n -> p (y q n)"), identh[:, :])
                    mm.then_inc(tp_ready, 1)

            pe.wait_ge(reach_in, 1)
            pe.transpose(ps[:, 4 * BANK:4 * BANK + P128], reach[:, :], identf[:, :]).then_inc(reach_t, 1)
            pe.wait_ge(reach_col, 1)
            pe.matmul(ps[0:1, 5 * BANK:5 * BANK + P128], reach_c[:, 1:2], identf[:, :],
                      start=True, stop=True).then_inc(reach_row, 1)

            pe.wait_ge(px_ready, 16 * (1 + NPART * B * 2))
            pe.wait_ge(reach_ready, 2)

            def distance(b, y):
                w = sel[:, ds(b, 1), :].rearrange("p a n -> p (a n)")
                first = BANK // W
                for k0, k1 in ((0, first), (first, KK)):
                    mm = pe.matmul(dist_ps[:, k0 * W:k1 * W], w, px[:, k0:k1, ds(y * W, W)],
                                   start=True, stop=True)
                mm.then_inc(dist_made, 1)

            def z_row(b, n, u):
                pe.wait_ge(zrow_staged, n + 1)
                pe.wait_ge(zrow_saved, n + (CREDIT - 1))
                pe.matmul(z_ps(u), stage[:, u, 0, :], wz[:, ds(b, 1), :],
                          start=True, stop=True).then_inc(zrow_made, 1)

            distance(0, 0)
            pe.wait_ge(dist_ready, 1)
            distance(0, 1)
            with pe.Fori(0, B) as b:
                for j in range(ZLEAD):
                    z_row(b, b * ZSLOTS + j, j % 2)
                with pe.Fori(0, HH // 2) as iy:
                    y = iy * 2
                    for u in range(2):
                        pe.wait_ge(dist_ready, b * HH + y + (u + 2))
                        distance(b + (y + (u + 2)) // HH, (y + (u + 2)) % HH)
                        z_row(b, b * ZSLOTS + y + (ZLEAD + u), u)
                        pe.wait_ge(hx_ready, b * (2 * HH) + y * 2 + (2 * u + 2))
                        pe.wait_ge(g_used, b * HH + y + (u - 1 + CREDIT))
                        pe.wait_ge(zrow_saved, b * ZSLOTS + y + (u + 5 + CREDIT))
                        for h in range(2):
                            for i, k in enumerate(TAPS[h]):
                                mm = pe.matmul(g_ps(u, h)[:, i, :, :], hx[:, u, k, :],
                                               z_sb[:, ds(y + (u + k // 3), 3), k * C:(k + 1) * C],
                                               start=True, stop=True)
                        mm.then_inc(g_ready, 1)

            def far_tile(b, y, n):
                pe.wait_ge(dist_ready, n + (NT + 2))
                distance(b, y)

            def far_turn(b, y, row, sign, n):
                pe.wait_ge(far_staged, n * 6 + 6)
                for ky in range(3):
                    s = slice(ky * 3 * C, (ky + 1) * 3 * C)
                    mm = pe.matmul(z_ps(0)[:, s], far_x[:, ky, :],
                                   wz[:, ds(b, 1), s], start=True, stop=True)
                mm.then_inc(far_zmade, 1)
                pe.wait_ge(far_zsaved, n + 1)
                pe.wait_ge(far_used, n + CREDIT)
                for k in range(KK):
                    mm = pe.matmul(far_ps[:, k * C:(k + 1) * C], hx[:, 0, k, :],
                                   far_z[:, k * C:(k + 1) * C], start=True, stop=True)
                mm.then_inc(far_made, 1)

            pe.wait_ge(acc_ready, NT)
            far_rows(pe, far_tile, far_turn)

            pe.wait_ge(acc_final, 1)
            pe.wait_ge(dist_ready, NT + 2)
            for c in range(NCH):
                if c >= 2:
                    pe.wait_ge(outt_saved, c - 1)
                for i in range(4):
                    mm = pe.transpose(ps[:, (c % 2) * BANK + i * P128:(c % 2) * BANK + (i + 1) * P128],
                                      acc[:, 4 * c + i, :, :].rearrange("p b o -> p (b o)"), identf[:, :])
                mm.then_inc(outt_made, 1)
            pe.wait_ge(bst_ready, 1)
            pe.matmul(ps[:, 2 * BANK:2 * BANK + 1], avg4[:, :], col(MVB), start=True, stop=True)\
                .then_inc(bmean_ready, 1)
            pe.wait_ge(bvar_in, 1)
            pe.matmul(ps[:, 3 * BANK:3 * BANK + 1], avg4[:, :], col(SQ), start=True, stop=True)\
                .then_inc(bvar_ready, 1)

        @block.scalar
        def _(act):
            act.dma_start(vec[:, :], d["vec"]).then_inc(params_loaded, 16)
            act.dma_start(attm[:, :], d["attm"]).then_inc(params_loaded, 16)
            act.dma_start(attp[:, :, :], d["attp"]).then_inc(map_loaded, 16)
            act.dma_start(attt[:, :, :], d["attt"]).then_inc(map_loaded, 16)
            act.dma_start(rowm[:, :], d["rowm"]).then_inc(map_loaded, 16)
            act.dma_start(blkm[:, :, :], d["blkm"]).then_inc(map_loaded, 16)

            def root(i, n=P128, w=1):
                act.wait_ge(root_in, i + 1)
                act.activation(small[0:n, ROOT_OUT:ROOT_OUT + w], small[0:n, ROOT_IN:ROOT_IN + w],
                               ACT.Sqrt).then_inc(root_done, 1)

            root(0)
            root(1, MAP_ROWS, 2)
            root(2)
            act.wait_ge(bn0_ready, 1)
            with act.Fori(0, NCH // 2) as ic:
                c = ic * 2
                for u in range(2):
                    act.wait_ge(conv_ready, c + (u + 1))
                    act.activation(f_sb[:, ds((c + u) * BANK, BANK)], ps[:, u * BANK:(u + 1) * BANK],
                                   ACT.Identity, bias=col(BB), scale=col(BS)).then_inc(f_ready, 1)
            with act.Fori(0, NCH // 2) as ic:
                c = ic * 2
                for u in range(2):
                    act.wait_ge(map_ready, c + (u + 1))
                    act.wait_ge(sig_used, c + CREDIT)
                    act.activation(sig[:, u, :], ps[:, (4 + u) * BANK:(5 + u) * BANK], ACT.Sigmoid)\
                        .then_inc(sig_ready, 1)
            root(3)
            act.wait_ge(off_saved, HH + CREDIT)
            act.wait_ge(rbias_ready, 3)
            act.activation(mod_v, mod_v, ACT.Sigmoid).then_inc(mod_ready, 1)
            for r in range(3):
                act.activation(per_tile(hy[:, r, :]), oy_v, ACT.Abs, bias=rbias[:, r:r + 1])\
                    .then_inc(hya_ready, 1)
            with act.Fori(0, HH // 16) as iy:
                y = iy * 16
                for u in range(2):
                    act.wait_ge(tp_ready, y // 8 + (u + 1))
                    bank = ps[0:NPART * B * KK, (2 + u) * BANK:(3 + u) * BANK].bitcast(bf16)
                    dst = tpart[0:NPART * B * KK, :].rearrange("p (g y x) -> p g y x", g=2, x=W)
                    act.activation(dst[:, :, ds(y + 8 * u, 8), :],
                                   bank.rearrange("p (y g x) -> p g y x", y=8, g=2),
                                   ACT.Copy).then_inc(tp_saved, 1)

            def distance(t, u):
                act.wait_ge(dist_made, t + 1)
                act.activation(dist[:, u, :], dist_ps, ACT.Abs).then_inc(dist_ready, 1)

            def weights(t, u):
                act.wait_ge(dist_ready, t + 1)
                act.wait_ge(g_ready, t + (CREDIT - 1))
                for g in range(2):
                    s = slice(g * W, (g + 1) * W)
                    act.activation(hx[s, u, :, s], dist[s, u, :].rearrange("p (k x) -> p k x", k=KK),
                                   ACT.Relu, bias=rbias[s, 0:1], scale=-1.0).then_inc(hx_ready, 1)

            def save_z(n, slot, u):
                act.wait_ge(zrow_made, n + (1 + CREDIT))
                act.activation(z_sb[:, ds(slot, 1), :], z_ps(u), ACT.Copy).then_inc(zrow_saved, 1)

            act.wait_ge(hx_zeroed, 1)
            distance(0, 0)
            weights(0, 0)
            distance(1, 1)
            with act.Fori(0, B) as b:
                for j in range(ZLEAD):
                    save_z(b * ZSLOTS + j, j, j % 2)
                with act.Fori(0, HH // 2) as iy:
                    y = iy * 2
                    for u in range(2):
                        weights(b * HH + y + (u + 1), (u + 1) % 2)
                        save_z(b * ZSLOTS + y + (ZLEAD + u), y + (ZLEAD + u), u)
                        distance(b * HH + y + (u + 2), u)

            def far_tile(b, y, n):
                act.wait_ge(dist_made, n + (NT + 3))
                act.activation(dist[:, 0, :], dist_ps, ACT.Abs).then_inc(dist_ready, 1)
                act.wait_ge(dist_ready, n + (NT + 3))
                for g in range(2):
                    s = slice(g * W, (g + 1) * W)
                    act.activation(hx[s, 0, :, s], dist[s, 0, :].rearrange("p (k x) -> p k x", k=KK),
                                   ACT.Relu, bias=rbias[s, 0:1], scale=-1.0).then_inc(hx_ready, 1)

            def far_turn(b, y, row, sign, n):
                act.wait_ge(far_zmade, n + (1 + CREDIT))
                act.activation(far_z[:, :], z_ps(0), ACT.Copy).then_inc(far_zsaved, 1)

            act.wait_ge(reach_ready, 2)
            far_rows(act, far_tile, far_turn)

            for c in range(NCH):
                act.wait_ge(outt_made, c + 1)
                dst = out_t.rearrange("p (g y x) -> p g y x", g=2, x=W)
                act.activation(dst[:, :, 4 * c:4 * c + 4, :],
                               ps[:, (c % 2) * BANK:(c % 2 + 1) * BANK]
                               .rearrange("p (y g x) -> p g y x", y=4, g=2),
                               ACT.Identity, bias=vec[:, V_DBIAS:V_DBIAS + 1]).then_inc(outt_saved, 1)
            root(4)
            act.wait_ge(bnc_ready, 1)
            for c in range(NCH):
                act.activation(out_t[:, c * BANK:(c + 1) * BANK], out_t[:, c * BANK:(c + 1) * BANK],
                               ACT.Relu, bias=col(SH), scale=col(SC)).then_inc(relu_ready, 1)

        @block.vector
        def _(vector):
            links = 0
            roots = 0

            def chain(ins):
                nonlocal links
                links += 1
                ins.then_inc(vchain, 1)
                vector.wait_ge(vchain, links)

            def rstd(dst, var, eps):
                nonlocal roots
                n, w = dst.shape
                v, r, t = (small[0:n, i:i + w] for i in (ROOT_IN, ROOT_OUT, ROOT_TMP))
                vector.tensor_scalar(v, var, eps, None, ALU.add).then_inc(root_in, 1)
                roots += 1
                vector.wait_ge(root_done, roots)
                chain(vector.reciprocal(dst, r))
                chain(vector.tensor_tensor(t, dst, dst, ALU.mult))
                chain(vector.scalar_tensor_tensor(t, t, -0.5, v, ALU.mult, ALU.mult))
                chain(vector.scalar_tensor_tensor(dst, t, 1.5, dst, ALU.add, ALU.mult))

            for s_ in (far_zmade, far_used, f_ready, att_saved, sig_ready, sig_used, off_ready, off_saved, tp_saved,
                       zrow_made, zrow_saved, g_ready, g_used):
                vector.sem_inc(s_, CREDIT)
            for r in range(3):
                vector.memset(rbias[:, r:r + 1], 1.0 - r).then_inc(rbias_ready, 1)
            vector.wait_ge(params_loaded, 32)
            p_ = lambda i: vec[:, i:i + 1]
            rstd(col(BS), p_(V_VAR), BR_EPS)
            chain(vector.tensor_tensor(col(BS), col(BS), p_(V_GAMMA), ALU.mult))
            chain(vector.tensor_tensor(col(BB), p_(V_CB), p_(V_MEAN), ALU.subtract))
            vector.scalar_tensor_tensor(col(BB), col(BB), col(BS), p_(V_BETA), ALU.mult, ALU.add)\
                .then_inc(bn0_ready, 1)
            vector.tensor_scalar(attw[:, :], attm[:, :], p_(V_ATTW), None, ALU.mult)\
                .then_inc(attw_ready, 1)
            vector.wait_ge(map_loaded, 64)
            R = MAP_ROWS
            a_ = lambda i: attp[:, i, :]
            t0, t1 = small[0:R, T0:T0 + 2], small[0:R, T1:T1 + 2]
            s_att, u_ = small[0:R, 21:23], small[0:R, 23:25]
            M_ATT, M_GH, M_GW, M_PR, M_ONE = (rowm[:, i:i + 1] for i in range(5))
            rstd(s_att, a_(A_VAR), ATT_EPS)
            chain(vector.tensor_tensor(s_att, s_att, a_(A_GAMMA), ALU.mult))
            chain(vector.tensor_tensor(t0, a_(A_B), a_(A_MEAN), ALU.subtract))
            chain(vector.tensor_scalar(u_, t0, M_ONE, M_ATT, ALU.mult, ALU.add))
            chain(vector.scalar_tensor_tensor(u_, a_(A_WGH), M_GH, u_, ALU.mult, ALU.add))
            chain(vector.scalar_tensor_tensor(u_, a_(A_WGW), M_GW, u_, ALU.mult, ALU.add))
            chain(vector.tensor_tensor(u_, u_, s_att, ALU.mult))
            chain(vector.scalar_tensor_tensor(u_, a_(A_BETA), M_ONE, u_, ALU.mult, ALU.add))
            chain(vector.tensor_tensor(u_, u_, attt[:, 0, :], ALU.mult))
            chain(vector.tensor_scalar(t1, attt[:, 1, :], M_GH, None, ALU.mult))
            chain(vector.scalar_tensor_tensor(t1, attt[:, 1, :], M_GW, t1, ALU.mult, ALU.add))
            chain(vector.scalar_tensor_tensor(t1, attt[:, 1, :], M_PR, t1, ALU.mult, ALU.add))
            chain(vector.tensor_tensor(u_, u_, t1, ALU.add))
            chain(vector.tensor_scalar(mapw[:, :], blkm[:, 0, :], small[0:R, 23:24], None, ALU.mult))
            vector.scalar_tensor_tensor(mapw[:, :], blkm[:, 1, :], small[0:R, 24:25], mapw[:, :],
                                        ALU.mult, ALU.add).then_inc(mapw_ready, 1)

            for c in range(NCH):
                if c % 2 == 0:
                    vector.wait_ge(x_loaded[c // 2], 16)
                vector.bn_stats(stats[:, c, :], x_sb[:, c * BANK:(c + 1) * BANK]).then_inc(st_ready, 1)
            vector.wait_ge(st_ready, NCH)
            chain(vector.bn_aggr(small[:, MV:MV + 2], stats[:, :, :]))
            rstd(col(RSTD), col(MV + 1), GN_EPS)
            vector.wait_ge(xpad_zeroed, 1)
            inner = xpad[:, PAD_T:PAD_T + H, 1:1 + W]
            x3 = x_sb[:, :].rearrange("p (y x) -> p y x", y=H)
            vector.tensor_scalar(inner, x3, col(MV), col(RSTD), ALU.subtract, ALU.mult)\
                .then_inc(norm1, 1)

            vector.wait_ge(attpad_zeroed, 1)
            att3 = attpad.rearrange("p (r x) -> p r x", x=AR)
            with vector.Fori(0, NCH // 2) as ic:
                c = ic * 2
                for u in range(2):
                    vector.wait_ge(att_ready, c + (u + 1))
                    vector.tensor_copy(att3[:, ds((c + u) * CH_ROWS + 1, CH_ROWS), 1:1 + W],
                                       ps[0:B * 2, (2 + u) * BANK:(3 + u) * BANK]
                                       .rearrange("p (r x) -> p r x", x=W)).then_inc(att_saved, 1)

            with vector.Fori(0, NCH // 2) as ic:
                c = ic * 2
                for u in range(2):
                    xs = x_sb[:, ds((c + u) * BANK, BANK)]
                    vector.wait_ge(sig_ready, c + (u + 1 + CREDIT))
                    vector.scalar_tensor_tensor(prod[:, u, 0:BANK], sig[:, u, :], p_(V_SCALE),
                                                f_sb[:, ds((c + u) * BANK, BANK)],
                                                ALU.mult, ALU.mult).then_inc(sig_used, 1)
                    vector.wait_ge(sig_used, c + (u + 1 + CREDIT))
                    vector.tensor_tensor(xs, prod[:, u, 0:BANK], xs, ALU.add).then_inc(x1_ready, 1)
                    vector.wait_ge(x1_ready, c + (u + 1))
                    vector.bn_stats(stats[:, ds(c + u, 1), :], xs).then_inc(st_ready, 1)
            vector.wait_ge(st_ready, 2 * NCH)
            chain(vector.bn_aggr(small[:, MV2:MV2 + 2], stats[:, :, :]))
            rstd(col(RSTD2), col(MV2 + 1), GN_EPS)
            vector.tensor_scalar(inner, x3, col(MV2), col(RSTD2), ALU.subtract, ALU.mult)\
                .then_inc(norm2, 1)

            vector.wait_ge(late_loaded, 16 * NLATE)
            with vector.Fori(0, HH // 2) as iy:
                y = iy * 2
                for u in range(2):
                    vector.wait_ge(off_ready, y + (u + 1 + CREDIT))
                    vector.tensor_tensor(offs[:, ds(y + u, 1), :], ps[:, u * BANK:u * BANK + NCOL],
                                         offb[:, :], ALU.add).then_inc(off_saved, 1)
            vector.wait_ge(off_saved, HH + CREDIT)
            rest = per_tile(hyt)
            part = [parts[:, :, q, :].rearrange("p y (b k) -> p y b k", b=B) for q in range(NPART)]
            chain(vector.tensor_copy(part[0], ox_v))
            chain(vector.tensor_tensor(rest, ox_v, part[0], ALU.subtract))
            chain(vector.tensor_copy(part[1], rest))
            vector.tensor_tensor(part[2], rest, part[1], ALU.subtract).then_inc(parts_ready, 1)
            vector.tensor_reduce(reach[:, :].rearrange("p (y b) -> p y b", b=B), oy_v, AX.X, ALU.max,
                                 apply_absolute_value=True).then_inc(reach_in, 1)
            vector.wait_ge(reach_t, 1)
            chain(vector.tensor_reduce(reach_c[:, 0:1], ps[:, 4 * BANK:4 * BANK + P128], AX.X, ALU.max))
            chain(vector.tensor_scalar(reach_c[:, 1:2], reach_c[:, 0:1], float(FAR - 1), None, ALU.min))
            vector.scalar_tensor_tensor(reach_c[:, 1:2], reach_c[:, 0:1], 1.0, reach_c[:, 1:2],
                                        ALU.is_ge, ALU.mult).then_inc(reach_col, 1)
            vector.wait_ge(reach_row, 1)
            vector.tensor_copy(reach_i[:, :], ps[0:1, 5 * BANK:5 * BANK + P128]).then_inc(reach_ready, 1)
            vector.tensor_reduce(reach_b[:, :], ps[0:1, 5 * BANK:5 * BANK + P128]
                                 .rearrange("p (y b) -> p b y", b=B), AX.X, ALU.max)\
                .then_inc(reach_ready, 1)
            vector.wait_ge(mod_ready, 1)
            for r in range(3):
                vector.wait_ge(hya_ready, r + 1)
                chain(vector.tensor_scalar(hy[:, r, :], hy[:, r, :], -1.0, 0.0, ALU.add, ALU.min))
                chain(vector.scalar_tensor_tensor(per_tile(hy[:, r, :]), per_tile(hy[:, r, :]), -2.0,
                                                  mod_v, ALU.mult, ALU.mult))


            with vector.Fori(0, B) as b:
                with vector.Fori(0, HH // 2) as iy:
                    y = iy * 2
                    for u in range(2):
                        t = b * HH + y + u
                        wv = hy[:, :, ds(y * (B * KK) + b * KK + u * (B * KK), KK)]\
                            .rearrange("p r k -> p k r").unsqueeze(3).to_broadcast([P128, KK, 3, C])
                        vector.wait_ge(g_ready, b * HH + y + (u + 1 + CREDIT))
                        pv = prod[:, u, :].rearrange("p (k r o) -> p k r o", k=KK, r=3)
                        for h in range(2):
                            k0, k1 = TAPS[h][0], TAPS[h][-1] + 1
                            mul = vector.tensor_tensor(pv[:, k0:k1], g_ps(u, h), wv[:, k0:k1], ALU.mult)
                        mul.then_inc(g_used, 1)
                        vector.wait_ge(g_used, b * HH + y + (u + 1 + CREDIT))
                        vector.tensor_reduce(acc[:, ds(y + u, 1), ds(b, 1), :],
                                             prod[:, u, :].rearrange("p (n o) -> p o n", o=C),
                                             AX.X, ALU.add).then_inc(acc_ready, 1)

            def far_tile(b, y, n):
                vector.memset(far_r[:, :], 1.0).then_inc(far_turns, 1)

            def far_turn(b, y, row, sign, n):
                oy = offs[:, ds(y, 1), ds(b * NOFF, KK)].rearrange("p a k -> p (a k)")
                mod = offs[:, ds(y, 1), ds(b * NOFF + 2 * KK, KK)].rearrange("p a k -> p (a k)")
                if sign > 0:
                    vector.drain()
                    vector.tensor_scalar(far_r[:, :], far_r[:, :], 1.0, None, ALU.add)
                vector.drain()
                vector.tensor_scalar(far_w[:, :], oy, far_r[:, :], 2.0,
                                     ALU.subtract if sign > 0 else ALU.add, ALU.mult)
                vector.drain()
                vector.tensor_scalar(far_u[:, :], far_w[:, :], -1.0, -2.0, ALU.mult, ALU.add)
                vector.drain()
                vector.scalar_tensor_tensor(far_w[:, :], far_w[:, :], -2.0, far_u[:, :],
                                            ALU.add, ALU.max)
                vector.drain()
                vector.scalar_tensor_tensor(far_w[:, :], far_w[:, :], 0.0, mod, ALU.min, ALU.mult)
                vector.drain()
                vector.wait_ge(far_made, n + 1)
                vector.tensor_tensor(far_p[:, :].rearrange("p (k o) -> p k o", o=C),
                                     far_ps.rearrange("p (k o) -> p k o", o=C),
                                     far_w[:, :].unsqueeze(2).to_broadcast([P128, KK, C]),
                                     ALU.mult).then_inc(far_used, 1)
                vector.drain()
                vector.tensor_reduce(far_s[:, :], far_p[:, :].rearrange("p (k o) -> p o k", o=C),
                                     AX.X, ALU.add)
                vector.drain()
                here = acc[:, ds(y, 1), ds(b, 1), :].rearrange("p a c o -> p (a c o)")
                vector.tensor_tensor(here, here, far_s[:, :], ALU.subtract)
                vector.drain()

            vector.wait_ge(reach_ready, 2)
            vector.wait_ge(acc_ready, NT)
            far_rows(vector, far_tile, far_turn)
            vector.drain().then_inc(acc_final, 1)

            ot = out_t.rearrange("p (g y x) -> p g y x", g=2, x=W)
            for c in range(NCH):
                vector.wait_ge(outt_saved, c + 1)
                for g in range(2):
                    vector.bn_stats(bstats[:, 2 * c + g, :],
                                    ot[:, g, 4 * c:4 * c + 4, :].rearrange("p y x -> p (y x)"))\
                        .then_inc(st_ready, 1)
            vector.wait_ge(st_ready, 4 * NCH)
            chain(vector.bn_aggr(small[:, MVB:MVB + 2], bstats[:, :, :]))
            vector.tensor_copy(col(62), col(MVB)).then_inc(bst_ready, 1)
            vector.wait_ge(bmean_ready, 1)
            chain(vector.tensor_copy(col(MEANB), ps[:, 2 * BANK:2 * BANK + 1]))
            chain(vector.tensor_tensor(col(DB), col(MVB), col(MEANB), ALU.subtract))
            vector.scalar_tensor_tensor(col(SQ), col(DB), col(DB), col(MVB + 1), ALU.mult, ALU.add)\
                .then_inc(bvar_in, 1)
            vector.wait_ge(bvar_ready, 1)
            rstd(col(SC), ps[:, 3 * BANK:3 * BANK + 1], BN_EPS)
            chain(vector.tensor_tensor(col(SC), col(SC), p_(V_DGAMMA), ALU.mult))
            chain(vector.tensor_tensor(col(T0), col(MEANB), col(SC), ALU.mult))
            vector.tensor_tensor(col(SH), p_(V_DBETA), col(T0), ALU.subtract).then_inc(bnc_ready, 1)
            for c in range(NCH):
                s = slice(c * BANK, (c + 1) * BANK)
                vector.wait_ge(relu_ready, c + 1)
                vector.tensor_tensor(x_sb[:, s], x_sb[:, s], out_t[:, s], ALU.add)\
                    .then_inc(res_ready, 1)



def _lay_out(i):
    a = {k: np.asarray(v) for k, v in i.items()}
    L0 = lambda n: a["L0_conv_" + n]
    L1 = lambda n: a["L1_conv_" + n]
    f = np.float32

    def bf(v):
        return (np.ascontiguousarray(v, f).view(np.uint32) >> 16).astype(np.uint16)

    d = {"x": a["x"].reshape(P128, NPIX)}
    taps = lambda w: np.ascontiguousarray(w.reshape(w.shape[0], w.shape[1], KK))
    both = lambda n: np.concatenate([L0(n.replace("?", "a")), L0(n.replace("?", "b"))])
    d["w0"] = taps(both("conv_?_w")).transpose(1, 2, 0)
    cols = [both("conv_?_b"), both("bn_?_gamma"), both("bn_?_beta"), both("bn_?_mean"),
            both("bn_?_var"),
            np.concatenate([L0("att_a_w")[0, :BR, 0, 0], L0("att_b_w")[0, :BR, 0, 0]]),
            np.concatenate([np.broadcast_to(L0("scale1"), (BR,)), np.broadcast_to(L0("scale2"), (BR,))]),
            L1("bias"), L1("gamma"), L1("beta")]
    d["vec"] = np.tile(np.stack(cols, 1), (B, 1))
    ow, ob = L1("offset_w"), L1("offset_b")
    d["woff"] = taps(np.concatenate([ow[0::2], ow[1::2], L1("mod_w")])).transpose(1, 2, 0)
    d["offb"] = np.tile(np.concatenate([ob[0::2], ob[1::2], L1("mod_b")]), (P128, B))
    d["wz"] = taps(L1("weight")).transpose(1, 2, 0).reshape(C, KW)
    per = [[L0(f"att_{s}_w")[0, BR, 0, 0], L0(f"att_{s}_w")[0, BR + 1, 0, 0], L0(f"att_{s}_b")[0],
            L0(f"att_bn_{s}_gamma")[0], L0(f"att_bn_{s}_beta")[0], L0(f"att_bn_{s}_mean")[0],
            L0(f"att_bn_{s}_var")[0]] for s in "ab"]
    d["attp"] = np.tile(np.array(per, f).T[None], (MAP_ROWS, 1, 1))
    tap = np.concatenate([np.repeat(np.arange(KK), B * 2), np.repeat(np.arange(KK), 4)])
    chan = np.concatenate([np.zeros(ATT_ROWS, int), np.tile([1, 2, 3, 0], KK)])
    attn = np.stack([taps(L0("attn_a_w"))[0], taps(L0("attn_b_w"))[0]])
    d["attt"] = np.stack([attn[:, 0, tap], attn[:, chan, tap]]).transpose(2, 0, 1)
    kind = np.concatenate([np.zeros(ATT_ROWS, int), np.tile([1, 2, 3, 4], KK)])
    d["rowm"] = (kind[:, None] == np.arange(5)).astype(f)
    p = np.arange(P128)
    pb, pbr = p // C, (p % C) // BR
    rb = np.concatenate([np.tile(np.repeat(np.arange(B), 2), KK), np.full(POS_ROWS, -1)])
    rbr = np.concatenate([np.tile([0, 1], KK * B), np.full(POS_ROWS, -1)])
    m = np.stack([(pbr == s)[None] & ((rb[:, None] == -1) | ((rb[:, None] == pb) & (rbr[:, None] == s)))
                  for s in range(2)], 1)
    d["blkm"] = m.astype(f)
    q = np.arange(B * 2)
    d["attm"] = ((q[None] // 2 == pb[:, None]) & (q[None] % 2 == pbr[:, None])).astype(f)
    gh = np.abs(np.arange(H, dtype=f) - H // 2 + f(0.5)) / f(H // 2)
    gw = np.abs(np.arange(W, dtype=f) - W // 2 + f(0.5)) / f(W // 2)
    GHt, GWt = np.broadcast_to(gh[:, None], (H, W)), np.broadcast_to(gw[None], (H, W))
    pr = np.sqrt(GHt ** 2 + GWt ** 2)
    k = f(2.0) / (pr.max() - pr.min())
    pr = k * pr + (f(1.0) - pr.max() * k)
    pos = np.zeros((4, AR, AR), f)
    pos[:, 1:1 + H, 1:1 + W] = np.stack([GHt, GWt, pr, np.ones((H, W), f)])
    flat = np.concatenate([pos.reshape(4, AR * AR), np.zeros((4, 2 * AR), f)], 1)
    d["pos"] = np.concatenate([flat[:, (t // 3) * AR + t % 3:][:, :IMLEN] for t in range(KK)])
    d["avg4"] = ((p[:, None] % C) == (p[None] % C)).astype(f) / f(B)
    d["identf"] = np.eye(P128, dtype=f)
    d["identh"] = bf(np.eye(P128))
    sel = np.zeros((SELK, B + 1, P128), f)
    for b in range(B):
        for part in range(NPART):
            for g in range(2):
                sel[2 * (part * B + b) + g, b, g * W:(g + 1) * W] = 1
        sel[SELK - 2, b] = 1
        sel[SELK - 1, b] = -(p % W)
    d["sel"] = bf(sel)
    xk = np.arange(W)[None] + (np.arange(KK) % 3 - 1)[:, None]
    prow = np.ones((2, KK, HH, W), f)
    prow[0] = xk[:, None, :]
    d["prow"] = bf(prow.reshape(2, KK, HH * W))
    return {n: np.ascontiguousarray(v) for n, v in d.items()}


def kernel(**inputs):
    import concourse.bacc as bacc
    from concourse.bass_utils import run_bass_kernel_spmd as run

    data = _lay_out(inputs)
    nc = bacc.Bacc("TRN2", target_bir_lowering=False, num_devices=1)
    arrays, aps = {}, {}
    for name, v in data.items():
        arrays[f"in_{name}"] = v
        aps[name] = nc.dram_tensor(f"in_{name}", v.shape, mybir.dt.from_np(v.dtype),
                                   kind="ExternalInput").ap()
    out = nc.dram_tensor("out", (P128, NPIX), mybir.dt.float32, kind="ExternalOutput").ap()
    conv_deform_kernel(nc, aps, out)
    r = run(nc, [arrays], core_ids=[0])
    return r.results[0]["out"].reshape(B, C, H, W)
```

```python
import concourse.bass as bass
from concourse import mybir
from contextlib import ExitStack
import numpy as np

B, C, H, W = 4, 32, 64, 64
NPIX = H * W
KK = 9
BR = C // 2
P128 = B * C
PAD_T = 2
XR, XC = H + 6, W + 2
AR = H + 2
CH_ROWS = 8
NCH = H // CH_ROWS
HH = H // 2
NQ = HH // CH_ROWS
NT = B * HH
NOFF = 27
NCOL = B * NOFF
ATT_ROWS = KK * B * 2
POS_ROWS = KK * 4
MAP_ROWS = ATT_ROWS + POS_ROWS
IMLEN = H * AR
NPART = 3
NXP = NPART * B
SELK = NXP * 2 + 2
KW = KK * C
G3 = 3 * C
GW = KK * G3
ZLEAD = 6
ZSLOTS = HH + ZLEAD
MAP_PARTS = ((0, 4, 5), (4, 6, 7), (6, 8, 8))
BR_EPS, ATT_EPS, GN_EPS, BN_EPS = 1e-3, 1e-5, 1e-5, 1e-5
BANK = 512
CREDIT = 4

V_CB, V_GAMMA, V_BETA, V_MEAN, V_VAR, V_ATTW, V_SCALE, V_DBIAS, V_DGAMMA, V_DBETA = range(10)
A_WGH, A_WGW, A_B, A_GAMMA, A_BETA, A_MEAN, A_VAR = range(7)


def conv_deform_kernel(nc, d, out):
    f32 = mybir.dt.float32
    bf16 = mybir.dt.bfloat16
    ALU = mybir.AluOpType
    ACT = mybir.ActivationFunctionType
    AX = mybir.AxisListType
    ds = bass.ds

    ctx = ExitStack()
    with ctx:
        def sb(name, shape, dt=f32):
            return ctx.enter_context(nc.sbuf_tensor(name, shape, dt))

        def sem(name):
            return ctx.enter_context(nc.semaphore(name))

        x_sb = sb("x_sb", [P128, NPIX])
        xpad = sb("xpad", [P128, XR, XC])
        woff = sb("woff", [P128, KK, NCOL])
        wz = sb("wz", [P128, B, KW])
        vec = sb("vec", [P128, 10])
        attp = sb("attp", [MAP_ROWS, 7, 2])
        attt = sb("attt", [MAP_ROWS, 2, 2])
        rowm = sb("rowm", [MAP_ROWS, 5])
        attm = sb("attm", [P128, B * 2])
        attw = sb("attw", [P128, B * 2])
        offb = sb("offb", [P128, NCOL])
        rbias = sb("rbias", [P128, 3])
        warm = sb("warm", [P128, 6])
        bstats = sb("bstats", [P128, 2 * NCH, 6])
        avg4 = sb("avg4", [P128, P128])
        identf = sb("identf", [P128, P128])
        identh = sb("identh", [P128, P128], bf16)
        sel = sb("sel", [SELK, B + 1, P128], bf16)
        small = sb("small", [P128, 64])
        stats = sb("stats", [P128, NCH, 6])
        offs = sb("offs", [P128, HH, NCOL])
        hy = sb("hy", [P128, 3, HH * B * KK])
        stage = sb("stage", [P128, 4, 3, 2 * W])
        dist = sb("dist", [P128, 2, KK * W])
        hx = sb("hx", [P128, 2, KK, 2 * W])
        prod = sb("prod", [P128, 2, GW])
        reach = sb("reach", [P128, HH * B])
        reach_c = sb("reach_c", [P128, 2])
        reach_i = sb("reach_i", [1, NT], mybir.dt.int32)
        far_code = sb("far_code", [1, 2, 2 * NT])
        tile_code = sb("tile_code", [1, NT])
        next_far = sb("next_far", [1, NT + 1], mybir.dt.int32)
        far_r = sb("far_r", [P128, 1])
        far_w = sb("far_w", [P128, KK])
        far_u = sb("far_u", [P128, KK])
        far_s = sb("far_s", [P128, C])
        zreg = sb("zreg", [P128, ZSLOTS, KW])
        preg = sb("preg", [P128, KK * HH * W], bf16)
        areg = sb("areg", [P128, NPIX])
        wreg = sb("wreg", [P128, NPIX // 2])

        w0 = wreg[:, 0:KK * P128].rearrange("p (k m) -> p k m", k=KK)
        blkm = wreg[0:MAP_ROWS, KK * P128:(KK + 2) * P128].rearrange("p (s m) -> p s m", s=2)
        mapw = wreg[0:MAP_ROWS, (KK + 2) * P128:(KK + 3) * P128]
        tpart = wreg[:, :].bitcast(bf16)
        far_x = wreg[:, 0:3 * P128].rearrange("p (k m) -> p k m", k=3)
        far_z = wreg[:, 3 * P128:3 * P128 + KW]
        far_p = wreg[:, 3 * P128 + KW:3 * P128 + 2 * KW]
        z_sb = zreg
        zflat = zreg[:, :, :].rearrange("p a n -> p (a n)")
        attpad = zflat[0:B * 2, 0:AR * AR]
        im2col = zflat[0:MAP_ROWS, AR * AR:AR * AR + IMLEN]
        out_t = zflat[:, 0:NPIX]
        f_sb = preg[:, 0:2 * NPIX].bitcast(f32)
        px = preg[0:SELK, :].rearrange("p (k n) -> p k n", k=KK)
        acc = areg[:, :].rearrange("p (y b o) -> p y b o", y=HH, b=B)
        parts = areg[:, NPIX // 2:NPIX // 2 + HH * NPART * B * KK // 2].bitcast(bf16)\
            .rearrange("p (y k q b) -> p y k q b", y=HH, k=KK, q=NPART)
        sig = dist[:, :, 0:BANK]
        hyt = prod[:, :, :].rearrange("p a n -> p (a n)")[:, 0:HH * B * KK]
        ps = ctx.enter_context(nc.psum_tensor("ps", [P128, 8 * BANK], f32))

        x_loaded = [sem(f"x_loaded{i}") for i in range(4)]
        w0_zeroed = sem("w0_zeroed")
        zeroed = sem("zeroed")
        w0_loaded = sem("w0_loaded")
        params_loaded = sem("params_loaded")
        map_loaded = sem("map_loaded")
        late_loaded = sem("late_loaded")
        vchain = sem("vchain")
        st_ready = sem("st_ready")
        pool_turns = sem("pool_turns")
        warmed = sem("warmed")
        warm_in = sem("warm_in")
        root_in = sem("root_in")
        root_done = sem("root_done")
        x1_ready = sem("x1_ready")
        rbias_ready = sem("rbias_ready")
        xpad_zeroed = sem("xpad_zeroed")
        attpad_zeroed = sem("attpad_zeroed")
        norm1 = sem("norm1")
        bn0_ready = sem("bn0_ready")
        attw_ready = sem("attw_ready")
        mapw_ready = sem("mapw_ready")
        conv_ready = sem("conv_ready")
        f_ready = sem("f_ready")
        att_ready = sem("att_ready")
        att_saved = sem("att_saved")
        pos_loaded = sem("pos_loaded")
        im2col_ready = [sem(f"im2col_ready{i}") for i in range(len(MAP_PARTS))]
        map_ready = sem("map_ready")
        sig_ready = sem("sig_ready")
        sig_used = sem("sig_used")
        norm2 = sem("norm2")
        first_staged = sem("first_staged")
        row_staged = sem("row_staged")
        hx_zeroed = sem("hx_zeroed")
        hx_ready = sem("hx_ready")
        off_ready = sem("off_ready")
        off_saved = sem("off_saved")
        parts_ready = sem("parts_ready")
        tp_ready = sem("tp_ready")
        tp_saved = sem("tp_saved")
        px_ready = sem("px_ready")
        mod_ready = sem("mod_ready")
        hya_ready = sem("hya_ready")
        hy_ready = sem("hy_ready")
        quarter_link = sem("quarter_link")
        zrow_staged = sem("zrow_staged")
        zrow_made = sem("zrow_made")
        zrow_saved = sem("zrow_saved")
        dist_made = sem("dist_made")
        dist_ready = sem("dist_ready")
        g_ready = sem("g_ready")
        g_used = sem("g_used")
        acc_ready = sem("acc_ready")
        acc_final = sem("acc_final")
        outt_made = sem("outt_made")
        outt_saved = sem("outt_saved")
        bst_ready = sem("bst_ready")
        bmean_ready = sem("bmean_ready")
        bvar_in = sem("bvar_in")
        bvar_ready = sem("bvar_ready")
        bnc_ready = sem("bnc_ready")
        relu_ready = sem("relu_ready")
        res_ready = sem("res_ready")
        stored = sem("stored")
        reach_in = sem("reach_in")
        reach_t = sem("reach_t")
        reach_col = sem("reach_col")
        reach_row = sem("reach_row")
        reach_read = sem("reach_read")
        reach_ready = sem("reach_ready")
        far_staged = sem("far_staged")
        far_zmade = sem("far_zmade")
        far_zsaved = sem("far_zsaved")
        far_made = sem("far_made")
        far_used = sem("far_used")
        far_turns = sem("far_turns")

        offv = offs[:, :, :].rearrange("p y (b j k) -> p y b j k", b=B, j=3)
        oy_v, ox_v, mod_v = (offv[:, :, :, j, :] for j in range(3))

        def per_tile(ap):
            return ap.rearrange("p (y b k) -> p y b k", y=HH, b=B)

        dist_ps = ps[:, 0:KK * W]

        TAPS = (range(0, BANK // G3), range(BANK // G3, KK))

        def g_ps(u, h):
            at = (2 + 2 * u + h) * BANK
            return ps[:, at:at + len(TAPS[h]) * G3].rearrange("p (k r o) -> p k r o", r=3, o=C)

        tp_ps = ps[0:NPART * B * KK, 4 * BANK:5 * BANK].bitcast(bf16)
        far_ps = ps[:, 2 * BANK:2 * BANK + KW]

        def z_ps(u):
            return ps[:, (6 + u) * BANK:(6 + u) * BANK + KW]

        def pair(row):
            return xpad[:, ds(row, 2, step=HH), :]

        def col(i, n=P128):
            return small[0:n, i:i + 1]

        MV, RSTD, BS, BB, MV2, RSTD2, MVB, SQ, MEANB, DB, VARB, SC, SH, T0, T1 = \
            0, 2, 3, 4, 5, 7, 8, 10, 11, 12, 13, 14, 15, 16, 17
        ROOT_IN, ROOT_OUT, ROOT_TMP = 40, 44, 48
        PX_DMAS = 2 * KK
        NLATE = 2 * B + 5
        NORM1 = NCH // 2
        block = ctx.enter_context(nc.Block())

        FAR = H + 2
        FAR1 = 128

        def far_rows(eng, tile, turn):
            tiles, turns, code = (eng.alloc_register(n) for n in ("far_tiles", "far_turn", "far_code"))
            eng.reg_mov(tiles, 0)
            eng.reg_mov(turns, 0)
            eng.reg_load(code, next_far[0:1, 0:1])
            with eng.While(lambda: eng.snap(code, min_val=0, max_val=NT * FAR1) < NT * FAR1):
                now = eng.snap(code, min_val=0, max_val=NT * FAR1 - 1)
                t = eng.snap(now // FAR1, min_val=0, max_val=NT - 1)
                reach_t = eng.snap(now % FAR1, min_val=1, max_val=FAR)
                y, b = eng.snap(t // B, min_val=0, max_val=HH - 1), eng.snap(t % B, min_val=0, max_val=B - 1)
                tile(b, y, eng.snap(tiles, min_val=0, max_val=NT))
                eng.reg_add(tiles, tiles, 1)
                with eng.Fori(1, reach_t + 1) as e:
                    n = eng.snap(turns, min_val=0, max_val=2 * NT * FAR)
                    for i, sign in enumerate((1, -1)):
                        turn(b, y, e + 1, sign, n + i)
                    eng.reg_add(turns, turns, 2)
                eng.reg_load(code, next_far[0:1, ds(t + 1, 1)])

        @block.sync
        def _(sync):
            for q in range(4):
                n = NPIX // 4
                sync.dma_start(x_sb[:, q * n:(q + 1) * n], d["x"][:, q * n:(q + 1) * n])\
                    .then_inc(x_loaded[q], 16)
            sync.wait_ge(w0_zeroed, 1)
            for b in range(B):
                s = slice(b * C, (b + 1) * C)
                sync.dma_start(w0[s, :, s], d["w0"]).then_inc(w0_loaded, 16)
            sync.dma_start(im2col[ATT_ROWS:MAP_ROWS, :], d["pos"]).then_inc(pos_loaded, 16)
            sync.wait_ge(zeroed, 2)
            for b in range(B):
                s = slice(b * C, (b + 1) * C)
                sync.dma_start(woff[s, :, b * NOFF:(b + 1) * NOFF], d["woff"]).then_inc(late_loaded, 16)
                sync.dma_start(wz[s, b, :], d["wz"]).then_inc(late_loaded, 16)
            sync.dma_start(offb[:, :], d["offb"]).then_inc(late_loaded, 16)
            sync.dma_start(avg4[:, :], d["avg4"]).then_inc(late_loaded, 16)
            sync.dma_start(identf[:, :], d["identf"]).then_inc(late_loaded, 16)
            sync.dma_start(identh[:, :], d["identh"].bitcast(bf16)).then_inc(late_loaded, 16)
            sync.dma_start(sel[:, :, :], d["sel"].bitcast(bf16)).then_inc(late_loaded, 16)
            for i, (c0, c1, saved) in enumerate(MAP_PARTS):
                sync.wait_ge(att_saved, saved + CREDIT)
                n0, n1 = c0 * CH_ROWS * AR, min(c1 * CH_ROWS * AR, IMLEN - 2)
                for t in range(KK):
                    o = (t // 3) * AR + t % 3
                    sync.dma_start(im2col[t * B * 2:(t + 1) * B * 2, n0:n1],
                                   attpad[:, o + n0:o + n1]).then_inc(im2col_ready[i], 16)
            sync.wait_ge(sig_used, NCH + CREDIT)
            sync.dma_start(px[SELK - 2:SELK, :, :], d["prow"].bitcast(bf16)).then_inc(px_ready, 16)
            n = CH_ROWS * W
            for q in range(NQ):
                sync.wait_ge(px_ready, 16 * (1 + q * PX_DMAS))
                sync.wait_ge(tp_saved, q + 1 + CREDIT)
                for g in range(2):
                    for k in range(KK):
                        sync.dma_start(px[g * NXP:(g + 1) * NXP, k, q * n:(q + 1) * n],
                                       tpart[k * NXP:(k + 1) * NXP,
                                             g * HH * W + q * n:g * HH * W + (q + 1) * n])\
                            .then_inc(px_ready, 16)
            for c in range(NCH):
                sync.wait_ge(res_ready, c + 1)
                sync.dma_start(out[:, c * BANK:(c + 1) * BANK], x_sb[:, c * BANK:(c + 1) * BANK])\
                    .then_inc(stored, 16)
            sync.wait_ge(stored, 16 * NCH)

        @block.gpsimd
        def _(pool):
            pool.memset(w0[:, :, :], 0.0).then_inc(w0_zeroed, 1)
            pool.memset(xpad[:, :, :], 0.0).then_inc(xpad_zeroed, 1)
            pool.memset(woff[:, :, :], 0.0).then_inc(zeroed, 1)
            pool.memset(wz[:, :, :], 0.0).then_inc(zeroed, 1)
            pool.memset(attpad, 0.0).then_inc(attpad_zeroed, 1)
            pool.memset(hx[:, :, :, :], 0.0).then_inc(hx_zeroed, 1)
            def stage_row(slot, row):
                for dx in range(3):
                    pool.tensor_copy(stage[:, slot, dx, :].rearrange("p (g x) -> p g x", g=2),
                                     pair(row)[:, :, dx:dx + W]).then_inc(row_staged, 1)

            pool.wait_ge(norm2, 2)
            for row in (2, 3, 4):
                pool.wait_ge(off_ready, row - 2 + CREDIT)
                stage_row(row % 4, row + PAD_T)
            pool.wait_ge(norm2, 4)
            with pool.Fori(1, HH // 4) as iy:
                y = iy * 4
                for u in range(4):
                    pool.wait_ge(off_ready, y + (u - 1 + CREDIT))
                    pool.sem_inc(pool_turns, 1)
                    stage_row((u + 1) % 4, y + (u + 1 + PAD_T))

            def stage_z(n, u, row):
                pool.wait_ge(zrow_made, n + (CREDIT - 1))
                pool.sem_inc(pool_turns, 1)
                pool.tensor_copy(stage[:, u, 0, :].rearrange("p (g x) -> p g x", g=2),
                                 pair(row)[:, :, 1:1 + W]).then_inc(zrow_staged, 1)

            pool.wait_ge(off_ready, HH + CREDIT)
            with pool.Fori(0, B) as b:
                with pool.Fori(0, ZSLOTS // 2) as iy:
                    for u in range(2):
                        stage_z(b * ZSLOTS + iy * 2 + u, u, iy * 2 + u)

            far_row = pool.alloc_register("far_row")

            def far_stage(b, y, row, sign, n):
                pool.wait_ge(far_zmade, n + CREDIT)
                pool.sem_inc(pool_turns, 1)
                for ky in range(3):
                    for g in range(2):
                        at = y + (g * HH + ky - 1 + PAD_T) + (row if sign > 0 else row * -1)
                        pool.reg_alu(far_row, at + FAR, FAR + PAD_T - 1, ALU.max)
                        pool.reg_alu(far_row, far_row, FAR + PAD_T + H, ALU.min)
                        pool.reg_alu(far_row, far_row, FAR, ALU.subtract)
                        r = pool.snap(far_row, min_val=PAD_T - 1, max_val=PAD_T + H)
                        pool.tensor_copy(far_x[:, ky, g * W:(g + 1) * W],
                                         xpad[:, ds(r, 1), 1:1 + W].rearrange("p a x -> p (a x)"))\
                            .then_inc(far_staged, 1)

            pool.wait_ge(reach_ready, 2)
            pool.wait_ge(px_ready, 16 * (1 + NQ * PX_DMAS))
            far_rows(pool, lambda b, y, n: None, far_stage)

        @block.tensor
        def _(pe):
            pe.wait_ge(norm1, 1)
            pe.wait_ge(w0_loaded, 16 * B)

            def conv_chunk(c, u):
                for t in range(KK):
                    rows = xpad[:, ds(c * CH_ROWS + (PAD_T - 1 + t // 3), CH_ROWS), t % 3:t % 3 + W]
                    mm = pe.matmul(ps[:, u * BANK:(u + 1) * BANK], w0[:, t, :], rows,
                                   start=t == 0, stop=t == KK - 1)
                mm.then_inc(conv_ready, 1)

            def att_chunk(c, u):
                pe.wait_ge(f_ready, c + (1 + CREDIT))
                pe.wait_ge(att_saved, c + (CREDIT - 1))
                pe.matmul(ps[0:B * 2, (2 + u) * BANK:(3 + u) * BANK], attw[:, :],
                          f_sb[:, ds(c * BANK, BANK)], start=True, stop=True).then_inc(att_ready, 1)

            def map_chunk(c, u):
                pe.wait_ge(sig_ready, c + (CREDIT - 1))
                rows = im2col[:, ds(c * (CH_ROWS * AR), CH_ROWS * AR)]\
                    .rearrange("p (r x) -> p r x", x=AR)[:, :, 0:W]
                pe.matmul(ps[:, (4 + u) * BANK:(5 + u) * BANK], mapw[:, :], rows,
                          start=True, stop=True).then_inc(map_ready, 1)

            conv_chunk(0, 0)
            pe.wait_ge(attw_ready, 1)
            with pe.Fori(0, NCH // 2 - 1) as ic:
                c = ic * 2
                for u in range(2):
                    if u == 0:
                        pe.wait_ge(norm1, ic + 1)
                    pe.wait_ge(f_ready, c + (u + CREDIT))
                    conv_chunk(c + (u + 1), 1 - u)
                    att_chunk(c + u, u)
            pe.wait_ge(mapw_ready, 1)
            pe.wait_ge(pos_loaded, 16)
            pe.wait_ge(im2col_ready[0], 16 * KK)
            for c in range(MAP_PARTS[0][0], MAP_PARTS[0][1]):
                map_chunk(c, c % 2)
            att_chunk(NCH - 2, 0)
            pe.wait_ge(norm1, NORM1)
            pe.wait_ge(f_ready, NCH - 2 + CREDIT)
            conv_chunk(NCH - 1, 1)
            att_chunk(NCH - 1, 1)
            for i in (1, 2):
                pe.wait_ge(im2col_ready[i], 16 * KK)
                for c in range(MAP_PARTS[i][0], MAP_PARTS[i][1]):
                    map_chunk(c, c % 2)

            pe.wait_ge(late_loaded, 16 * NLATE)

            def conv_quarter(q):
                for u in range(CH_ROWS):
                    rows = q * (3 * CH_ROWS) + u * 3
                    if not (isinstance(rows, int) and rows == 0):
                        pe.wait_ge(row_staged, rows)
                    pe.wait_ge(off_saved, q * CH_ROWS + (u - 4 + CREDIT + 1))
                    for t in range(KK):
                        mm = pe.matmul(ps[:, (u % 4) * BANK:(u % 4) * BANK + NCOL],
                                       stage[:, (u + t // 3 - 1) % 4, t % 3, :],
                                       woff[:, t, :], start=t == 0, stop=t == KK - 1)
                    mm.then_inc(off_ready, 1)

            def parts_quarter(q):
                pe.wait_ge(parts_ready, q + 1)
                pe.wait_ge(tp_saved, q + CREDIT)
                for i in range(CH_ROWS):
                    mm = pe.transpose(tp_ps[:, i * P128:(i + 1) * P128],
                                      parts[:, ds(q * CH_ROWS + i, 1), :, :, :]
                                      .rearrange("p y k q b -> p (y k q b)"), identh[:, :])
                mm.then_inc(tp_ready, 1)

            pe.wait_ge(first_staged, 9)
            conv_quarter(0)
            with pe.Fori(1, NQ) as q:
                conv_quarter(q)
                parts_quarter(q - 1)
            pe.wait_ge(reach_in, NQ)
            pe.transpose(ps[:, 6 * BANK:6 * BANK + P128], reach[:, :], identf[:, :]).then_inc(reach_t, 1)
            parts_quarter(NQ - 1)
            pe.wait_ge(reach_col, 1)
            pe.matmul(ps[0:1, 7 * BANK:7 * BANK + P128], reach_c[:, 1:2], identf[:, :],
                      start=True, stop=True).then_inc(reach_row, 1)

            pe.wait_ge(reach_read, 1)

            def px_wait(y):
                pe.wait_ge(px_ready, (y // CH_ROWS) * (16 * PX_DMAS) + 16 * (1 + PX_DMAS))

            def distance(b, y):
                w = sel[:, ds(b, 1), :].rearrange("p a n -> p (a n)")
                first = BANK // W
                for k0, k1 in ((first, KK), (0, first)):
                    mm = pe.matmul(dist_ps[:, k0 * W:k1 * W], w, px[:, k0:k1, ds(y * W, W)],
                                   start=True, stop=True)
                mm.then_inc(dist_made, 1)

            def z_row(b, n, u):
                pe.wait_ge(zrow_staged, n + 1)
                pe.wait_ge(zrow_saved, n + (CREDIT - 1))
                pe.matmul(z_ps(u), stage[:, u, 0, :], wz[:, ds(b, 1), :],
                          start=True, stop=True).then_inc(zrow_made, 1)

            px_wait(0)
            distance(0, 0)
            pe.wait_ge(dist_ready, 1)
            distance(0, 1)
            with pe.Fori(0, B) as b:
                for j in range(ZLEAD):
                    z_row(b, b * ZSLOTS + j, j % 2)
                with pe.Fori(0, HH // 2) as iy:
                    y = iy * 2
                    for u in range(2):
                        pe.wait_ge(dist_ready, b * HH + y + (u + 2))
                        px_wait((y + (u + 2)) % HH)
                        distance(b + (y + (u + 2)) // HH, (y + (u + 2)) % HH)
                        z_row(b, b * ZSLOTS + y + (ZLEAD + u), u)
                        pe.wait_ge(hx_ready, b * (2 * HH) + y * 2 + (2 * u + 2))
                        pe.wait_ge(g_used, b * HH + y + (u - 1 + CREDIT))
                        pe.wait_ge(zrow_saved, b * ZSLOTS + y + (u + 5 + CREDIT))
                        for h in range(2):
                            for i, k in enumerate(TAPS[h]):
                                mm = pe.matmul(g_ps(u, h)[:, i, :, :], hx[:, u, k, :],
                                               z_sb[:, ds(y + (u + k // 3), 3), k * C:(k + 1) * C],
                                               start=True, stop=True)
                        mm.then_inc(g_ready, 1)

            def far_tile(b, y, n):
                pe.wait_ge(dist_ready, n + (NT + 2))
                distance(b, y)

            def far_turn(b, y, row, sign, n):
                pe.wait_ge(far_staged, n * 6 + 6)
                for ky in range(3):
                    s = slice(ky * 3 * C, (ky + 1) * 3 * C)
                    mm = pe.matmul(z_ps(0)[:, s], far_x[:, ky, :],
                                   wz[:, ds(b, 1), s], start=True, stop=True)
                mm.then_inc(far_zmade, 1)
                pe.wait_ge(far_zsaved, n + 1)
                pe.wait_ge(far_used, n + CREDIT)
                for k in range(KK):
                    mm = pe.matmul(far_ps[:, k * C:(k + 1) * C], hx[:, 0, k, :],
                                   far_z[:, k * C:(k + 1) * C], start=True, stop=True)
                mm.then_inc(far_made, 1)

            pe.wait_ge(acc_ready, NT)
            pe.wait_ge(px_ready, 16 * (1 + NQ * PX_DMAS))
            far_rows(pe, far_tile, far_turn)

            pe.wait_ge(acc_final, 1)
            pe.wait_ge(dist_ready, NT + 2)
            for c in range(NCH):
                if c >= 2:
                    pe.wait_ge(outt_saved, c - 1)
                for i in range(4):
                    mm = pe.transpose(ps[:, (c % 2) * BANK + i * P128:(c % 2) * BANK + (i + 1) * P128],
                                      acc[:, 4 * c + i, :, :].rearrange("p b o -> p (b o)"), identf[:, :])
                mm.then_inc(outt_made, 1)
            pe.wait_ge(bst_ready, 1)
            pe.matmul(ps[:, 2 * BANK:2 * BANK + 1], avg4[:, :], col(MVB), start=True, stop=True)\
                .then_inc(bmean_ready, 1)
            pe.wait_ge(bvar_in, 1)
            pe.matmul(ps[:, 3 * BANK:3 * BANK + 1], avg4[:, :], col(SQ), start=True, stop=True)\
                .then_inc(bvar_ready, 1)

        @block.scalar
        def _(act):
            act.wait_ge(warm_in, 1)
            act.activation(warm[:, 1:2], warm[:, 0:1], ACT.Sqrt).then_inc(warmed, 1)
            act.dma_start(vec[:, :], d["vec"]).then_inc(params_loaded, 16)
            act.dma_start(attm[:, :], d["attm"]).then_inc(params_loaded, 16)
            act.dma_start(attp[:, :, :], d["attp"]).then_inc(map_loaded, 16)
            act.dma_start(attt[:, :, :], d["attt"]).then_inc(map_loaded, 16)
            act.dma_start(rowm[:, :], d["rowm"]).then_inc(map_loaded, 16)
            act.dma_start(blkm[:, :, :], d["blkm"]).then_inc(map_loaded, 16)
            act.dma_start(tile_code[:, :], d["tcode"]).then_inc(map_loaded, 16)

            def root(i, n=P128, w=1):
                act.wait_ge(root_in, i + 1)
                act.activation(small[0:n, ROOT_OUT:ROOT_OUT + w], small[0:n, ROOT_IN:ROOT_IN + w],
                               ACT.Sqrt).then_inc(root_done, 1)

            root(0)
            root(1)
            root(2, MAP_ROWS, 2)
            act.activation(warm[:, 2:3], warm[:, 0:1], ACT.Sigmoid).then_inc(warmed, 1)
            act.wait_ge(bn0_ready, 1)

            def save_branches(c, u):
                act.wait_ge(conv_ready, c + 1)
                act.activation(f_sb[:, ds(c * BANK, BANK)], ps[:, u * BANK:(u + 1) * BANK],
                               ACT.Identity, bias=col(BB), scale=col(BS)).then_inc(f_ready, 1)

            def sigmoid_map(c, u):
                act.wait_ge(map_ready, c + 1)
                act.wait_ge(sig_used, c + (CREDIT - 1))
                act.activation(sig[:, u, :], ps[:, (4 + u) * BANK:(5 + u) * BANK], ACT.Sigmoid)\
                    .then_inc(sig_ready, 1)

            with act.Fori(0, NCH // 2 - 1) as ic:
                for u in range(2):
                    save_branches(ic * 2 + u, u)
            save_branches(NCH - 2, 0)
            for c in range(MAP_PARTS[0][1]):
                sigmoid_map(c, c % 2)
            save_branches(NCH - 1, 1)
            for c in range(MAP_PARTS[0][1], NCH):
                sigmoid_map(c, c % 2)
            act.activation(warm[:, 3:4], warm[:, 0:1], ACT.Sqrt).then_inc(warmed, 1)
            root(3)
            act.activation(warm[:, 4:5], warm[:, 0:1], ACT.Sigmoid).then_inc(warmed, 1)
            act.wait_ge(rbias_ready, 3)
            with act.Fori(0, NQ) as q:
                rows = ds(q * CH_ROWS, CH_ROWS)
                act.wait_ge(off_saved, q * CH_ROWS + (CH_ROWS + CREDIT))
                act.activation(mod_v[:, rows], mod_v[:, rows], ACT.Sigmoid).then_inc(mod_ready, 1)
                for r in range(3):
                    act.activation(per_tile(hy[:, r, :])[:, rows], oy_v[:, rows], ACT.Abs,
                                   bias=rbias[:, r:r + 1]).then_inc(hya_ready, 1)
                act.wait_ge(tp_ready, q + 1)
                dst = tpart[0:NPART * B * KK, :].rearrange("p (g y x) -> p g y x", g=2, x=W)
                act.activation(dst[:, :, rows, :], tp_ps.rearrange("p (y g x) -> p g y x", y=CH_ROWS, g=2),
                               ACT.Copy).then_inc(tp_saved, 1)

            def distance(t, u):
                act.wait_ge(dist_made, t + 1)
                act.activation(dist[:, u, :], dist_ps, ACT.Abs).then_inc(dist_ready, 1)

            def weights(t, u):
                act.wait_ge(dist_ready, t + 1)
                act.wait_ge(g_ready, t + (CREDIT - 1))
                for g in range(2):
                    s = slice(g * W, (g + 1) * W)
                    act.activation(hx[s, u, :, s], dist[s, u, :].rearrange("p (k x) -> p k x", k=KK),
                                   ACT.Relu, bias=rbias[s, 0:1], scale=-1.0).then_inc(hx_ready, 1)

            def save_z(n, slot, u):
                act.wait_ge(zrow_made, n + (1 + CREDIT))
                act.activation(z_sb[:, ds(slot, 1), :], z_ps(u), ACT.Copy).then_inc(zrow_saved, 1)

            act.wait_ge(hx_zeroed, 1)
            distance(0, 0)
            weights(0, 0)
            distance(1, 1)
            with act.Fori(0, B) as b:
                for j in range(ZLEAD):
                    save_z(b * ZSLOTS + j, j, j % 2)
                with act.Fori(0, HH // 2) as iy:
                    y = iy * 2
                    for u in range(2):
                        weights(b * HH + y + (u + 1), (u + 1) % 2)
                        save_z(b * ZSLOTS + y + (ZLEAD + u), y + (ZLEAD + u), u)
                        distance(b * HH + y + (u + 2), u)

            def far_tile(b, y, n):
                act.wait_ge(dist_made, n + (NT + 3))
                act.activation(dist[:, 0, :], dist_ps, ACT.Abs).then_inc(dist_ready, 1)
                act.wait_ge(dist_ready, n + (NT + 3))
                for g in range(2):
                    s = slice(g * W, (g + 1) * W)
                    act.activation(hx[s, 0, :, s], dist[s, 0, :].rearrange("p (k x) -> p k x", k=KK),
                                   ACT.Relu, bias=rbias[s, 0:1], scale=-1.0).then_inc(hx_ready, 1)

            def far_turn(b, y, row, sign, n):
                act.wait_ge(far_zmade, n + (1 + CREDIT))
                act.activation(far_z[:, :], z_ps(0), ACT.Copy).then_inc(far_zsaved, 1)

            act.wait_ge(reach_ready, 2)
            far_rows(act, far_tile, far_turn)

            act.activation(warm[:, 5:6], warm[:, 0:1], ACT.Sqrt).then_inc(warmed, 1)
            for c in range(NCH):
                act.wait_ge(outt_made, c + 1)
                dst = out_t.rearrange("p (g y x) -> p g y x", g=2, x=W)
                act.activation(dst[:, :, 4 * c:4 * c + 4, :],
                               ps[:, (c % 2) * BANK:(c % 2 + 1) * BANK]
                               .rearrange("p (y g x) -> p g y x", y=4, g=2),
                               ACT.Identity, bias=vec[:, V_DBIAS:V_DBIAS + 1]).then_inc(outt_saved, 1)
            root(4)
            act.wait_ge(bnc_ready, 1)
            for c in range(NCH):
                act.activation(out_t[:, c * BANK:(c + 1) * BANK], out_t[:, c * BANK:(c + 1) * BANK],
                               ACT.Relu, bias=col(SH), scale=col(SC)).then_inc(relu_ready, 1)

        @block.vector
        def _(vector):
            links = 0
            roots = 0

            def chain(ins):
                nonlocal links
                links += 1
                ins.then_inc(vchain, 1)
                vector.wait_ge(vchain, links)

            def rstd(dst, var, eps):
                nonlocal roots
                n, w = dst.shape
                v, r, t = (small[0:n, i:i + w] for i in (ROOT_IN, ROOT_OUT, ROOT_TMP))
                vector.tensor_scalar(v, var, eps, None, ALU.add).then_inc(root_in, 1)
                roots += 1
                vector.wait_ge(root_done, roots)
                chain(vector.reciprocal(dst, r))
                chain(vector.tensor_tensor(t, dst, dst, ALU.mult))
                chain(vector.scalar_tensor_tensor(t, t, -0.5, v, ALU.mult, ALU.mult))
                chain(vector.scalar_tensor_tensor(dst, t, 1.5, dst, ALU.add, ALU.mult))

            vector.memset(warm[:, :], 1.0).then_inc(warm_in, 1)
            for s_ in (far_zmade, far_used, f_ready, att_saved, sig_ready, sig_used, off_ready, off_saved, tp_saved,
                       zrow_made, zrow_saved, g_ready, g_used):
                vector.sem_inc(s_, CREDIT)
            for r in range(3):
                vector.memset(rbias[:, r:r + 1], 1.0 - r).then_inc(rbias_ready, 1)
            for c in range(NCH):
                if c % 2 == 0:
                    vector.wait_ge(x_loaded[c // 2], 16)
                vector.bn_stats(stats[:, c, :], x_sb[:, c * BANK:(c + 1) * BANK]).then_inc(st_ready, 1)
            vector.wait_ge(st_ready, NCH)
            chain(vector.bn_aggr(small[:, MV:MV + 2], stats[:, :, :]))
            rstd(col(RSTD), col(MV + 1), GN_EPS)
            vector.wait_ge(xpad_zeroed, 1)
            inner = xpad[:, PAD_T:PAD_T + H, 1:1 + W]
            x3 = x_sb[:, :].rearrange("p (y x) -> p y x", y=H)
            ends = [0] + [min((2 * i + 3) * CH_ROWS + 1, H) for i in range(NORM1)]
            for r0, r1 in zip(ends[:-1], ends[1:]):
                vector.tensor_scalar(inner[:, r0:r1, :], x3[:, r0:r1, :], col(MV), col(RSTD),
                                     ALU.subtract, ALU.mult).then_inc(norm1, 1)

            vector.wait_ge(params_loaded, 32)
            p_ = lambda i: vec[:, i:i + 1]
            rstd(col(BS), p_(V_VAR), BR_EPS)
            chain(vector.tensor_tensor(col(BS), col(BS), p_(V_GAMMA), ALU.mult))
            chain(vector.tensor_tensor(col(BB), p_(V_CB), p_(V_MEAN), ALU.subtract))
            vector.scalar_tensor_tensor(col(BB), col(BB), col(BS), p_(V_BETA), ALU.mult, ALU.add)\
                .then_inc(bn0_ready, 1)
            vector.tensor_scalar(attw[:, :], attm[:, :], p_(V_ATTW), None, ALU.mult)\
                .then_inc(attw_ready, 1)
            vector.wait_ge(map_loaded, 80)
            R = MAP_ROWS
            a_ = lambda i: attp[:, i, :]
            t0, t1 = small[0:R, T0:T0 + 2], small[0:R, T1:T1 + 2]
            s_att, u_ = small[0:R, 21:23], small[0:R, 23:25]
            M_ATT, M_GH, M_GW, M_PR, M_ONE = (rowm[:, i:i + 1] for i in range(5))
            rstd(s_att, a_(A_VAR), ATT_EPS)
            chain(vector.tensor_tensor(s_att, s_att, a_(A_GAMMA), ALU.mult))
            chain(vector.tensor_tensor(t0, a_(A_B), a_(A_MEAN), ALU.subtract))
            chain(vector.tensor_scalar(u_, t0, M_ONE, M_ATT, ALU.mult, ALU.add))
            chain(vector.scalar_tensor_tensor(u_, a_(A_WGH), M_GH, u_, ALU.mult, ALU.add))
            chain(vector.scalar_tensor_tensor(u_, a_(A_WGW), M_GW, u_, ALU.mult, ALU.add))
            chain(vector.tensor_tensor(u_, u_, s_att, ALU.mult))
            chain(vector.scalar_tensor_tensor(u_, a_(A_BETA), M_ONE, u_, ALU.mult, ALU.add))
            chain(vector.tensor_tensor(u_, u_, attt[:, 0, :], ALU.mult))
            chain(vector.tensor_scalar(t1, attt[:, 1, :], M_GH, None, ALU.mult))
            chain(vector.scalar_tensor_tensor(t1, attt[:, 1, :], M_GW, t1, ALU.mult, ALU.add))
            chain(vector.scalar_tensor_tensor(t1, attt[:, 1, :], M_PR, t1, ALU.mult, ALU.add))
            chain(vector.tensor_tensor(u_, u_, t1, ALU.add))
            chain(vector.tensor_scalar(mapw[:, :], blkm[:, 0, :], small[0:R, 23:24], None, ALU.mult))
            vector.scalar_tensor_tensor(mapw[:, :], blkm[:, 1, :], small[0:R, 24:25], mapw[:, :],
                                        ALU.mult, ALU.add).then_inc(mapw_ready, 1)

            vector.wait_ge(attpad_zeroed, 1)
            att3 = attpad.rearrange("p (r x) -> p r x", x=AR)

            def save_att(c, u):
                vector.wait_ge(att_ready, c + 1)
                vector.tensor_copy(att3[:, ds(c * CH_ROWS + 1, CH_ROWS), 1:1 + W],
                                   ps[0:B * 2, (2 + u) * BANK:(3 + u) * BANK]
                                   .rearrange("p (r x) -> p r x", x=W)).then_inc(att_saved, 1)

            def add_branches(c):
                xs = [x_sb[:, (c + u) * BANK:(c + u + 1) * BANK] for u in range(2)]
                for u in range(2):
                    vector.wait_ge(sig_ready, c + u + 1 + CREDIT)
                    vector.scalar_tensor_tensor(prod[:, u, 0:BANK], sig[:, u, :], p_(V_SCALE),
                                                f_sb[:, (c + u) * BANK:(c + u + 1) * BANK],
                                                ALU.mult, ALU.mult).then_inc(sig_used, 1)
                for u in range(2):
                    vector.wait_ge(sig_used, c + u + 1 + CREDIT)
                    vector.tensor_tensor(xs[u], prod[:, u, 0:BANK], xs[u], ALU.add).then_inc(x1_ready, 1)
                for u in range(2):
                    vector.wait_ge(x1_ready, c + u + 1)
                    vector.bn_stats(stats[:, c + u, :], xs[u]).then_inc(st_ready, 1)

            with vector.Fori(0, NCH // 2 - 1) as ic:
                for u in range(2):
                    save_att(ic * 2 + u, u)
            add_branches(0)
            save_att(NCH - 2, 0)
            add_branches(2)
            save_att(NCH - 1, 1)
            for c in range(MAP_PARTS[0][1], NCH, 2):
                add_branches(c)
            vector.wait_ge(st_ready, 2 * NCH)
            chain(vector.bn_aggr(small[:, MV2:MV2 + 2], stats[:, :, :]))
            rstd(col(RSTD2), col(MV2 + 1), GN_EPS)
            pieces2 = ((0, CH_ROWS), (HH - 1, HH + CH_ROWS), (CH_ROWS, HH - 1), (HH + CH_ROWS, H))
            for i, (r0, r1) in enumerate(pieces2):
                vector.tensor_scalar(inner[:, r0:r1, :], x3[:, r0:r1, :], col(MV2),
                                     col(RSTD2), ALU.subtract, ALU.mult).then_inc(norm2, 1)
                if i == 1:
                    vector.wait_ge(norm2, 2)
                    for slot, row in ((3, PAD_T - 1), (0, PAD_T), (1, PAD_T + 1)):
                        for dx in range(3):
                            vector.tensor_copy(stage[:, slot, dx, :].rearrange("p (g x) -> p g x", g=2),
                                               pair(row)[:, :, dx:dx + W]).then_inc(first_staged, 1)

            vector.wait_ge(late_loaded, 16 * NLATE)
            links_q = 6

            def link(ins, q, n):
                ins.then_inc(quarter_link, 1)
                vector.wait_ge(quarter_link, q * links_q + (n + 1))

            def offsets(q):
                y = q * CH_ROWS
                for u in range(CH_ROWS):
                    vector.wait_ge(off_ready, y + (u + 1 + CREDIT))
                    vector.tensor_tensor(offs[:, ds(y + u, 1), :],
                                         ps[:, (u % 4) * BANK:(u % 4) * BANK + NCOL],
                                         offb[:, :], ALU.add).then_inc(off_saved, 1)
                vector.wait_ge(off_saved, y + (CH_ROWS + CREDIT))
                rows = ds(y, CH_ROWS)
                vector.tensor_reduce(reach[:, :].rearrange("p (y b) -> p y b", b=B)[:, rows],
                                     oy_v[:, rows], AX.X, ALU.max,
                                     apply_absolute_value=True).then_inc(reach_in, 1)
                rest = hyt[:, 0:CH_ROWS * B * KK].rearrange("p (y b k) -> p y b k", y=CH_ROWS, b=B)
                part = [parts[:, rows, :, i, :].rearrange("p y k b -> p y b k") for i in range(NPART)]
                link(vector.tensor_copy(part[0], ox_v[:, rows]), q, 0)
                link(vector.tensor_tensor(rest, ox_v[:, rows], part[0], ALU.subtract), q, 1)
                link(vector.tensor_copy(part[1], rest), q, 2)
                vector.tensor_tensor(part[2], rest, part[1], ALU.subtract).then_inc(parts_ready, 1)

            def vertical_weights(q):
                rows = ds(q * CH_ROWS, CH_ROWS)
                vector.wait_ge(mod_ready, q + 1)
                for r in range(3):
                    hyr = per_tile(hy[:, r, :])[:, rows]
                    vector.wait_ge(hya_ready, q * 3 + (r + 1))
                    link(vector.tensor_scalar(hyr, hyr, -1.0, 0.0, ALU.add, ALU.min), q, 3 + r)
                    vector.scalar_tensor_tensor(hyr, hyr, -2.0, mod_v[:, rows], ALU.mult, ALU.mult)\
                        .then_inc(hy_ready, 1)

            with vector.Fori(0, NQ - 1) as q:
                offsets(q)
                vertical_weights(q)
            offsets(NQ - 1)
            vector.wait_ge(reach_t, 1)
            chain(vector.tensor_reduce(reach_c[:, 0:1], ps[:, 6 * BANK:6 * BANK + P128], AX.X, ALU.max))
            chain(vector.tensor_scalar(reach_c[:, 1:2], reach_c[:, 0:1], float(FAR - 1), None, ALU.min))
            vector.scalar_tensor_tensor(reach_c[:, 1:2], reach_c[:, 0:1], 1.0, reach_c[:, 1:2],
                                        ALU.is_ge, ALU.mult).then_inc(reach_col, 1)
            vector.wait_ge(reach_row, 1)
            vector.tensor_copy(reach_i[:, :], ps[0:1, 7 * BANK:7 * BANK + P128]).then_inc(reach_read, 1)
            vertical_weights(NQ - 1)
            vector.wait_ge(reach_read, 1)
            chain(vector.tensor_copy(far_code[:, 1, 0:NT], reach_i[:, :]))
            chain(vector.memset(far_code[:, 0, :], float(FAR1 * NT)))
            chain(vector.tensor_tensor(tile_code[:, :], tile_code[:, :], far_code[:, 1, 0:NT], ALU.add))
            chain(vector.scalar_tensor_tensor(far_code[:, 0, 0:NT], far_code[:, 1, 0:NT], 1.0,
                                              tile_code[:, :], ALU.min, ALU.mult))
            chain(vector.tensor_scalar(far_code[:, 0, 0:NT], far_code[:, 0, 0:NT], float(FAR1 * NT),
                                       None, ALU.add))
            chain(vector.memset(far_code[:, 1, NT:2 * NT], float(FAR1 * NT)))
            for i in range(7):
                a_, b_ = far_code[:, i % 2, :], far_code[:, 1 - i % 2, :]
                chain(vector.tensor_tensor(b_[:, 0:NT], a_[:, 0:NT], a_[:, 1 << i:NT + (1 << i)], ALU.min))
            vector.tensor_copy(next_far[:, :], far_code[:, 1, 0:NT + 1]).then_inc(reach_ready, 2)
            vector.wait_ge(hy_ready, NQ * 3)
            with vector.Fori(0, B) as b:
                with vector.Fori(0, HH // 2) as iy:
                    y = iy * 2
                    for u in range(2):
                        t = b * HH + y + u
                        wv = hy[:, :, ds(y * (B * KK) + b * KK + u * (B * KK), KK)]\
                            .rearrange("p r k -> p k r").unsqueeze(3).to_broadcast([P128, KK, 3, C])
                        vector.wait_ge(g_ready, b * HH + y + (u + 1 + CREDIT))
                        pv = prod[:, u, :].rearrange("p (k r o) -> p k r o", k=KK, r=3)
                        for h in range(2):
                            k0, k1 = TAPS[h][0], TAPS[h][-1] + 1
                            mul = vector.tensor_tensor(pv[:, k0:k1], g_ps(u, h), wv[:, k0:k1], ALU.mult)
                        mul.then_inc(g_used, 1)
                        vector.wait_ge(g_used, b * HH + y + (u + 1 + CREDIT))
                        vector.tensor_reduce(acc[:, ds(y + u, 1), ds(b, 1), :],
                                             prod[:, u, :].rearrange("p (n o) -> p o n", o=C),
                                             AX.X, ALU.add).then_inc(acc_ready, 1)

            def far_tile(b, y, n):
                vector.memset(far_r[:, :], 1.0).then_inc(far_turns, 1)

            def far_turn(b, y, row, sign, n):
                oy = offs[:, ds(y, 1), ds(b * NOFF, KK)].rearrange("p a k -> p (a k)")
                mod = offs[:, ds(y, 1), ds(b * NOFF + 2 * KK, KK)].rearrange("p a k -> p (a k)")
                if sign > 0:
                    vector.drain()
                    vector.tensor_scalar(far_r[:, :], far_r[:, :], 1.0, None, ALU.add)
                vector.drain()
                vector.tensor_scalar(far_w[:, :], oy, far_r[:, :], 2.0,
                                     ALU.subtract if sign > 0 else ALU.add, ALU.mult)
                vector.drain()
                vector.tensor_scalar(far_u[:, :], far_w[:, :], -1.0, -2.0, ALU.mult, ALU.add)
                vector.drain()
                vector.scalar_tensor_tensor(far_w[:, :], far_w[:, :], -2.0, far_u[:, :],
                                            ALU.add, ALU.max)
                vector.drain()
                vector.scalar_tensor_tensor(far_w[:, :], far_w[:, :], 0.0, mod, ALU.min, ALU.mult)
                vector.drain()
                vector.wait_ge(far_made, n + 1)
                vector.tensor_tensor(far_p[:, :].rearrange("p (k o) -> p k o", o=C),
                                     far_ps.rearrange("p (k o) -> p k o", o=C),
                                     far_w[:, :].unsqueeze(2).to_broadcast([P128, KK, C]),
                                     ALU.mult).then_inc(far_used, 1)
                vector.drain()
                vector.tensor_reduce(far_s[:, :], far_p[:, :].rearrange("p (k o) -> p o k", o=C),
                                     AX.X, ALU.add)
                vector.drain()
                here = acc[:, ds(y, 1), ds(b, 1), :].rearrange("p a c o -> p (a c o)")
                vector.tensor_tensor(here, here, far_s[:, :], ALU.subtract)
                vector.drain()

            vector.wait_ge(reach_ready, 2)
            vector.wait_ge(acc_ready, NT)
            far_rows(vector, far_tile, far_turn)
            vector.drain().then_inc(acc_final, 1)

            ot = out_t.rearrange("p (g y x) -> p g y x", g=2, x=W)
            for c in range(NCH):
                vector.wait_ge(outt_saved, c + 1)
                for g in range(2):
                    vector.bn_stats(bstats[:, 2 * c + g, :],
                                    ot[:, g, 4 * c:4 * c + 4, :].rearrange("p y x -> p (y x)"))\
                        .then_inc(st_ready, 1)
            vector.wait_ge(st_ready, 4 * NCH)
            chain(vector.bn_aggr(small[:, MVB:MVB + 2], bstats[:, :, :]))
            vector.tensor_copy(col(62), col(MVB)).then_inc(bst_ready, 1)
            vector.wait_ge(bmean_ready, 1)
            chain(vector.tensor_copy(col(MEANB), ps[:, 2 * BANK:2 * BANK + 1]))
            chain(vector.tensor_tensor(col(DB), col(MVB), col(MEANB), ALU.subtract))
            vector.scalar_tensor_tensor(col(SQ), col(DB), col(DB), col(MVB + 1), ALU.mult, ALU.add)\
                .then_inc(bvar_in, 1)
            vector.wait_ge(bvar_ready, 1)
            rstd(col(SC), ps[:, 3 * BANK:3 * BANK + 1], BN_EPS)
            chain(vector.tensor_tensor(col(SC), col(SC), p_(V_DGAMMA), ALU.mult))
            chain(vector.tensor_tensor(col(T0), col(MEANB), col(SC), ALU.mult))
            vector.tensor_tensor(col(SH), p_(V_DBETA), col(T0), ALU.subtract).then_inc(bnc_ready, 1)
            for c in range(NCH):
                s = slice(c * BANK, (c + 1) * BANK)
                vector.wait_ge(relu_ready, c + 1)
                vector.tensor_tensor(x_sb[:, s], x_sb[:, s], out_t[:, s], ALU.add)\
                    .then_inc(res_ready, 1)



def _lay_out(i):
    a = {k: np.asarray(v) for k, v in i.items()}
    L0 = lambda n: a["L0_conv_" + n]
    L1 = lambda n: a["L1_conv_" + n]
    f = np.float32

    def bf(v):
        return (np.ascontiguousarray(v, f).view(np.uint32) >> 16).astype(np.uint16)

    d = {"x": a["x"].reshape(P128, NPIX)}
    taps = lambda w: np.ascontiguousarray(w.reshape(w.shape[0], w.shape[1], KK))
    both = lambda n: np.concatenate([L0(n.replace("?", "a")), L0(n.replace("?", "b"))])
    d["w0"] = taps(both("conv_?_w")).transpose(1, 2, 0)
    cols = [both("conv_?_b"), both("bn_?_gamma"), both("bn_?_beta"), both("bn_?_mean"),
            both("bn_?_var"),
            np.concatenate([L0("att_a_w")[0, :BR, 0, 0], L0("att_b_w")[0, :BR, 0, 0]]),
            np.concatenate([np.broadcast_to(L0("scale1"), (BR,)), np.broadcast_to(L0("scale2"), (BR,))]),
            L1("bias"), L1("gamma"), L1("beta")]
    d["vec"] = np.tile(np.stack(cols, 1), (B, 1))
    ow, ob = L1("offset_w"), L1("offset_b")
    d["woff"] = taps(np.concatenate([ow[0::2], ow[1::2], L1("mod_w")])).transpose(1, 2, 0)
    d["offb"] = np.tile(np.concatenate([ob[0::2], ob[1::2], L1("mod_b")]), (P128, B))
    d["wz"] = taps(L1("weight")).transpose(1, 2, 0).reshape(C, KW)
    per = [[L0(f"att_{s}_w")[0, BR, 0, 0], L0(f"att_{s}_w")[0, BR + 1, 0, 0], L0(f"att_{s}_b")[0],
            L0(f"att_bn_{s}_gamma")[0], L0(f"att_bn_{s}_beta")[0], L0(f"att_bn_{s}_mean")[0],
            L0(f"att_bn_{s}_var")[0]] for s in "ab"]
    d["attp"] = np.tile(np.array(per, f).T[None], (MAP_ROWS, 1, 1))
    tap = np.concatenate([np.repeat(np.arange(KK), B * 2), np.repeat(np.arange(KK), 4)])
    chan = np.concatenate([np.zeros(ATT_ROWS, int), np.tile([1, 2, 3, 0], KK)])
    attn = np.stack([taps(L0("attn_a_w"))[0], taps(L0("attn_b_w"))[0]])
    d["attt"] = np.stack([attn[:, 0, tap], attn[:, chan, tap]]).transpose(2, 0, 1)
    kind = np.concatenate([np.zeros(ATT_ROWS, int), np.tile([1, 2, 3, 4], KK)])
    d["rowm"] = (kind[:, None] == np.arange(5)).astype(f)
    p = np.arange(P128)
    pb, pbr = p // C, (p % C) // BR
    rb = np.concatenate([np.tile(np.repeat(np.arange(B), 2), KK), np.full(POS_ROWS, -1)])
    rbr = np.concatenate([np.tile([0, 1], KK * B), np.full(POS_ROWS, -1)])
    m = np.stack([(pbr == s)[None] & ((rb[:, None] == -1) | ((rb[:, None] == pb) & (rbr[:, None] == s)))
                  for s in range(2)], 1)
    d["blkm"] = m.astype(f)
    q = np.arange(B * 2)
    d["attm"] = ((q[None] // 2 == pb[:, None]) & (q[None] % 2 == pbr[:, None])).astype(f)
    gh = np.abs(np.arange(H, dtype=f) - H // 2 + f(0.5)) / f(H // 2)
    gw = np.abs(np.arange(W, dtype=f) - W // 2 + f(0.5)) / f(W // 2)
    GHt, GWt = np.broadcast_to(gh[:, None], (H, W)), np.broadcast_to(gw[None], (H, W))
    pr = np.sqrt(GHt ** 2 + GWt ** 2)
    k = f(2.0) / (pr.max() - pr.min())
    pr = k * pr + (f(1.0) - pr.max() * k)
    pos = np.zeros((4, AR, AR), f)
    pos[:, 1:1 + H, 1:1 + W] = np.stack([GHt, GWt, pr, np.ones((H, W), f)])
    flat = np.concatenate([pos.reshape(4, AR * AR), np.zeros((4, 2 * AR), f)], 1)
    d["pos"] = np.concatenate([flat[:, (t // 3) * AR + t % 3:][:, :IMLEN] for t in range(KK)])
    d["avg4"] = ((p[:, None] % C) == (p[None] % C)).astype(f) / f(B)
    d["tcode"] = (128 * (np.arange(NT, dtype=f) - NT))[None]
    d["identf"] = np.eye(P128, dtype=f)
    d["identh"] = bf(np.eye(P128))
    sel = np.zeros((SELK, B + 1, P128), f)
    for b in range(B):
        for part in range(NPART):
            for g in range(2):
                sel[g * NXP + part * B + b, b, g * W:(g + 1) * W] = 1
        sel[SELK - 2, b] = 1
        sel[SELK - 1, b] = -(p % W)
    d["sel"] = bf(sel)
    xk = np.arange(W)[None] + (np.arange(KK) % 3 - 1)[:, None]
    prow = np.ones((2, KK, HH, W), f)
    prow[0] = xk[:, None, :]
    d["prow"] = bf(prow.reshape(2, KK, HH * W))
    return {n: np.ascontiguousarray(v) for n, v in d.items()}


def kernel(**inputs):
    import concourse.bacc as bacc
    from concourse.bass_utils import run_bass_kernel_spmd as run

    data = _lay_out(inputs)
    nc = bacc.Bacc("TRN2", target_bir_lowering=False, num_devices=1)
    arrays, aps = {}, {}
    for name, v in data.items():
        arrays[f"in_{name}"] = v
        aps[name] = nc.dram_tensor(f"in_{name}", v.shape, mybir.dt.from_np(v.dtype),
                                   kind="ExternalInput").ap()
    out = nc.dram_tensor("out", (P128, NPIX), mybir.dt.float32, kind="ExternalOutput").ap()
    conv_deform_kernel(nc, aps, out)
    r = run(nc, [arrays], core_ids=[0])
    return r.results[0]["out"].reshape(B, C, H, W)
```

```python
import concourse.bass as bass
from concourse import mybir
from contextlib import ExitStack
import numpy as np

B, C, H, W = 4, 32, 64, 64
NPIX = H * W
KK = 9
BR = C // 2
P128 = B * C
PAD_T = 2
XR, XC = H + 6, W + 2
AR = H + 2
CH_ROWS = 8
NCH = H // CH_ROWS
HH = H // 2
NQ = HH // CH_ROWS
NT = B * HH
NOFF = 27
NCOL = B * NOFF
ATT_ROWS = KK * B * 2
POS_ROWS = KK * 4
MAP_ROWS = ATT_ROWS + POS_ROWS
IMLEN = H * AR
NPART = 3
NXP = NPART * B
SELK = NXP * 2 + 2
KW = KK * C
G3 = 3 * C
GW = KK * G3
ZPIECE = 10
ZLEAD = 6
ZSLOTS = HH + ZLEAD
MAP_PARTS = ((0, 4, 5), (4, 6, 7), (6, 8, 8))
SYNC_TAPS = 6
X_ENDS = (0, 2, 4, 6, 7, 8)
BR_EPS, ATT_EPS, GN_EPS, BN_EPS = 1e-3, 1e-5, 1e-5, 1e-5
BANK = 512
CREDIT = 4

V_CB, V_GAMMA, V_BETA, V_MEAN, V_VAR, V_ATTW, V_SCALE, V_DBIAS, V_DGAMMA, V_DBETA = range(10)
A_WGH, A_WGW, A_B, A_GAMMA, A_BETA, A_MEAN, A_VAR = range(7)


def conv_deform_kernel(nc, d, scratch, out):
    f32 = mybir.dt.float32
    bf16 = mybir.dt.bfloat16
    ALU = mybir.AluOpType
    ACT = mybir.ActivationFunctionType
    AX = mybir.AxisListType
    ds = bass.ds

    ctx = ExitStack()
    with ctx:
        def sb(name, shape, dt=f32):
            return ctx.enter_context(nc.sbuf_tensor(name, shape, dt))

        def sem(name):
            return ctx.enter_context(nc.semaphore(name))

        x_sb = sb("x_sb", [P128, NPIX])
        xpad = sb("xpad", [P128, XR, XC])
        wz = sb("wz", [P128, B, KW])
        vec = sb("vec", [P128, 10])
        attp = sb("attp", [MAP_ROWS, 7, 2])
        attt = sb("attt", [MAP_ROWS, 2, 2])
        rowm = sb("rowm", [MAP_ROWS, 5])
        attm = sb("attm", [P128, B * 2])
        attw = sb("attw", [P128, B * 2])
        offb = sb("offb", [P128, NCOL])
        rbias = sb("rbias", [P128, 3])
        warm = sb("warm", [P128, 6])
        avg4 = sb("avg4", [P128, P128])
        identf = sb("identf", [P128, P128])
        identh = sb("identh", [P128, P128], bf16)
        sel = sb("sel", [SELK, B + 1, P128], bf16)
        small = sb("small", [P128, 64])
        stats = sb("stats", [P128, NCH, 6])
        offs = sb("offs", [P128, HH, NCOL])
        hy = sb("hy", [P128, 3, HH * B * KK])
        wzp = sb("wzp", [P128, 2, KW], bf16)
        dist = sb("dist", [P128, 2, KK * W])
        hx = sb("hx", [P128, 2, KK, 2 * W])
        prod = sb("prod", [P128, 2, GW])
        reach = sb("reach", [P128, HH * B])
        reach_c = sb("reach_c", [P128, 2])
        reach_i = sb("reach_i", [1, NT], mybir.dt.int32)
        far_code = sb("far_code", [1, 2, 2 * NT])
        tile_code = sb("tile_code", [1, NT])
        next_far = sb("next_far", [1, NT + 1], mybir.dt.int32)
        far_r = sb("far_r", [P128, 1])
        far_w = sb("far_w", [P128, KK, 2])
        far_u = sb("far_u", [P128, KK, 2])
        far_s = sb("far_s", [P128, C])
        zreg = sb("zreg", [P128, ZSLOTS, KW])
        preg = sb("preg", [P128, KK * HH * W], bf16)
        areg = sb("areg", [P128, NPIX])
        wreg = sb("wreg", [P128, NPIX // 2])
        sreg = sb("sreg", [P128, 4 * 3 * 2 * W + KK * NCOL])

        w0 = wreg[:, 0:KK * P128].rearrange("p (k m) -> p k m", k=KK)
        blkm = wreg[0:MAP_ROWS, KK * P128:(KK + 2) * P128].rearrange("p (s m) -> p s m", s=2)
        mapw = wreg[0:MAP_ROWS, (KK + 2) * P128:(KK + 3) * P128]
        tpart = wreg[:, :].bitcast(bf16)
        far_x = wreg[:, 0:6 * P128].rearrange("p (i k m) -> p i k m", i=2, k=3)
        far_z = wreg[:, 6 * P128:6 * P128 + 2 * KW].rearrange("p (i k o) -> p k i o", i=2, k=KK)
        far_p = wreg[:, 6 * P128 + 2 * KW:6 * P128 + 4 * KW].rearrange("p (k i o) -> p k i o", k=KK, i=2)
        stage = sreg[:, 0:12 * P128].rearrange("p (s x n) -> p s x n", s=4, x=3)
        woff = sreg[:, 12 * P128:12 * P128 + KK * NCOL].rearrange("p (k n) -> p k n", k=KK)
        xs_sb = sreg[:, 0:ZSLOTS * P128 // 2].bitcast(bf16)
        z_sb = zreg
        zflat = zreg[:, :, :].rearrange("p a n -> p (a n)")
        attpad = zflat[0:B * 2, 0:AR * AR]
        im2col = zflat[0:MAP_ROWS, AR * AR:AR * AR + IMLEN]
        wz_rep = zflat[:, AR * AR + IMLEN:AR * AR + IMLEN + KW]
        wz_rest = zflat[:, AR * AR + IMLEN + KW:AR * AR + IMLEN + 2 * KW]
        wz_parts = zflat[:, AR * AR + IMLEN + 2 * KW:AR * AR + IMLEN + 3 * KW + KW // 2].bitcast(bf16)\
            .rearrange("p (q n) -> p q n", q=3)
        xparts = zflat[:, ZSLOTS * KW - NPART * ZSLOTS * W:ZSLOTS * KW].bitcast(bf16)\
            .rearrange("p (q n) -> p q n", q=NPART)
        xrest = areg[:, 0:ZPIECE * P128]
        out_t = zflat[:, 0:NPIX]
        f_sb = preg[:, 0:2 * NPIX].bitcast(f32)
        px = preg[0:SELK, :].rearrange("p (k n) -> p k n", k=KK)
        acc = areg[:, :].rearrange("p (y b o) -> p y b o", y=HH, b=B)
        parts = areg[:, NPIX // 2:NPIX // 2 + HH * NPART * B * KK // 2].bitcast(bf16)\
            .rearrange("p (y k q b) -> p y k q b", y=HH, k=KK, q=NPART)
        sig = dist[:, :, 0:BANK]
        bstats = dist[:, 0, 0:2 * NCH * 6].rearrange("p (c s) -> p c s", s=6)
        hyt = prod[:, :, :].rearrange("p a n -> p (a n)")[:, 0:HH * B * KK]
        ps = ctx.enter_context(nc.psum_tensor("ps", [P128, 8 * BANK], f32))

        x_loaded = [sem(f"x_loaded{i}") for i in range(len(X_ENDS) - 1)]
        w0_zeroed = sem("w0_zeroed")
        zeroed = sem("zeroed")
        w0_loaded = sem("w0_loaded")
        params_loaded = sem("params_loaded")
        map_loaded = sem("map_loaded")
        late_loaded = sem("late_loaded")
        vchain = sem("vchain")
        st_ready = sem("st_ready")
        pool_turns = sem("pool_turns")
        load_turns = sem("load_turns")
        warmed = sem("warmed")
        warm_in = sem("warm_in")
        root_in = sem("root_in")
        root_done = sem("root_done")
        x1_ready = sem("x1_ready")
        rbias_ready = sem("rbias_ready")
        xpad_zeroed = sem("xpad_zeroed")
        attpad_zeroed = sem("attpad_zeroed")
        norm1 = sem("norm1")
        bn0_ready = sem("bn0_ready")
        attw_ready = sem("attw_ready")
        mapw_ready = sem("mapw_ready")
        conv_ready = sem("conv_ready")
        f_ready = sem("f_ready")
        att_ready = sem("att_ready")
        att_saved = sem("att_saved")
        pos_loaded = sem("pos_loaded")
        im2col_ready = [sem(f"im2col_ready{i}") for i in range(len(MAP_PARTS))]
        im2col_rest = sem("im2col_rest")
        map_ready = sem("map_ready")
        sig_ready = sem("sig_ready")
        sig_used = sem("sig_used")
        norm2 = sem("norm2")
        first_staged = sem("first_staged")
        second_staged = sem("second_staged")
        row_staged = sem("row_staged")
        hx_zeroed = sem("hx_zeroed")
        hx_ready = sem("hx_ready")
        off_ready = sem("off_ready")
        off_saved = sem("off_saved")
        parts_ready = sem("parts_ready")
        tp_ready = sem("tp_ready")
        tp_saved = sem("tp_saved")
        px_ready = sem("px_ready")
        mod_ready = sem("mod_ready")
        hya_ready = sem("hya_ready")
        hy_ready = sem("hy_ready")
        quarter_link = sem("quarter_link")
        split = sem("split")
        wz_loaded = sem("wz_loaded")
        wzp_ready = sem("wzp_ready")
        xparts_ready = sem("xparts_ready")
        xparts_stored = sem("xparts_stored")
        xs_loaded = sem("xs_loaded")
        zrow_made = sem("zrow_made")
        zrow_saved = sem("zrow_saved")
        lead_made = sem("lead_made")
        lead_saved = sem("lead_saved")
        dist_made = sem("dist_made")
        dist_ready = sem("dist_ready")
        g_ready = sem("g_ready")
        g_used = sem("g_used")
        acc_ready = sem("acc_ready")
        acc_final = sem("acc_final")
        outt_made = sem("outt_made")
        outt_saved = sem("outt_saved")
        bst_ready = sem("bst_ready")
        bmean_ready = sem("bmean_ready")
        bvar_in = sem("bvar_in")
        bvar_ready = sem("bvar_ready")
        bnc_ready = sem("bnc_ready")
        relu_ready = sem("relu_ready")
        res_ready = sem("res_ready")
        stored = sem("stored")
        reach_in = sem("reach_in")
        reach_t = sem("reach_t")
        reach_col = sem("reach_col")
        reach_row = sem("reach_row")
        reach_read = sem("reach_read")
        reach_ready = sem("reach_ready")
        far_staged = sem("far_staged")
        far_zmade = sem("far_zmade")
        far_zsaved = sem("far_zsaved")
        far_made = sem("far_made")
        far_used = sem("far_used")
        far_turns = sem("far_turns")

        offv = offs[:, :, :].rearrange("p y (b j k) -> p y b j k", b=B, j=3)
        oy_v, ox_v, mod_v = (offv[:, :, :, j, :] for j in range(3))

        def per_tile(ap):
            return ap.rearrange("p (y b k) -> p y b k", y=HH, b=B)

        def dist_ps(bank):
            return ps[:, bank * BANK:bank * BANK + KK * W]

        TAPS = (range(0, BANK // G3), range(BANK // G3, KK))

        def g_ps(u, h):
            at = (2 + 2 * u + h) * BANK
            return ps[:, at:at + len(TAPS[h]) * G3].rearrange("p (k r o) -> p k r o", r=3, o=C)

        tp_ps = ps[0:NPART * B * KK, 4 * BANK:5 * BANK].bitcast(bf16)
        far_ps = [ps[:, (2 + h) * BANK:(2 + h) * BANK + len(TAPS[h]) * 2 * C]
                  .rearrange("p (k i o) -> p k i o", i=2, o=C) for h in range(2)]

        def z_ps(u, bank=6):
            return ps[:, (bank + u) * BANK:(bank + u) * BANK + KW]

        LEAD_BANKS = (6, 6, 2, 2, 6, 6)

        def pair(row):
            return xpad[:, ds(row, 2, step=HH), :]

        def col(i, n=P128):
            return small[0:n, i:i + 1]

        MV, RSTD, BS, BB, MV2, RSTD2, MVB, SQ, MEANB, DB, SC, SH, T0, T1 = \
            0, 2, 3, 4, 5, 7, 8, 10, 11, 12, 14, 15, 16, 17
        ROOT_IN, ROOT_OUT, ROOT_TMP = 40, 44, 48
        PX_DMAS = 2 * KK
        NLATE = 2 * B + 5
        LOADS = [(q * CH_ROWS + (ZLEAD if q else 0), (q + 1) * CH_ROWS + ZLEAD) for q in range(NQ)]
        PIECES = [(q * ZPIECE, min((q + 1) * ZPIECE, ZSLOTS)) for q in range(NQ)]
        FIRST = 5
        NORM1 = NCH // 2 + 1
        block = ctx.enter_context(nc.Block())

        FAR = H + 2
        FAR1 = 128

        def far_rows(eng, tile, turn):
            tiles, turns, code = (eng.alloc_register(n) for n in ("far_tiles", "far_turn", "far_code"))
            eng.reg_mov(tiles, 0)
            eng.reg_mov(turns, 0)
            eng.reg_load(code, next_far[0:1, 0:1])
            with eng.While(lambda: eng.snap(code, min_val=0, max_val=NT * FAR1) < NT * FAR1):
                now = eng.snap(code, min_val=0, max_val=NT * FAR1 - 1)
                t = eng.snap(now // FAR1, min_val=0, max_val=NT - 1)
                reach_t = eng.snap(now % FAR1, min_val=1, max_val=FAR)
                y, b = eng.snap(t // B, min_val=0, max_val=HH - 1), eng.snap(t % B, min_val=0, max_val=B - 1)
                tile(b, y, eng.snap(tiles, min_val=0, max_val=NT))
                eng.reg_add(tiles, tiles, 1)
                with eng.Fori(1, reach_t + 1) as e:
                    turn(b, y, e + 1, eng.snap(turns, min_val=0, max_val=NT * FAR))
                    eng.reg_add(turns, turns, 1)
                eng.reg_load(code, next_far[0:1, ds(t + 1, 1)])

        @block.sync
        def _(sync):
            for i, (c0, c1) in enumerate(zip(X_ENDS[:-1], X_ENDS[1:])):
                sync.dma_start(x_sb[:, c0 * BANK:c1 * BANK], d["x"][:, c0 * BANK:c1 * BANK])\
                    .then_inc(x_loaded[i], 16)
            sync.wait_ge(w0_zeroed, 1)
            for b in range(B):
                s = slice(b * C, (b + 1) * C)
                sync.dma_start(w0[s, :, s], d["w0"]).then_inc(w0_loaded, 16)
            sync.dma_start(im2col[ATT_ROWS:MAP_ROWS, :], d["pos"]).then_inc(pos_loaded, 16)
            for i in range(4):
                sync.dma_start(wz_rep[i * C:(i + 1) * C, :], d["wz"]).then_inc(wz_loaded, 16)
            sync.wait_ge(zeroed, 2)
            for b in range(B):
                s = slice(b * C, (b + 1) * C)
                sync.dma_start(woff[s, :, b * NOFF:(b + 1) * NOFF], d["woff"]).then_inc(late_loaded, 16)
                sync.dma_start(wz[s, b, :], d["wz"]).then_inc(late_loaded, 16)
            sync.dma_start(offb[:, :], d["offb"]).then_inc(late_loaded, 16)
            sync.dma_start(avg4[:, :], d["avg4"]).then_inc(late_loaded, 16)
            sync.dma_start(identf[:, :], d["identf"]).then_inc(late_loaded, 16)
            sync.dma_start(identh[:, :], d["identh"].bitcast(bf16)).then_inc(late_loaded, 16)
            sync.dma_start(sel[:, :, :], d["sel"].bitcast(bf16)).then_inc(late_loaded, 16)
            for i, (c0, c1, saved) in enumerate(MAP_PARTS):
                sync.wait_ge(att_saved, saved + CREDIT)
                n0, n1 = c0 * CH_ROWS * AR, min(c1 * CH_ROWS * AR, IMLEN - 2)
                for t in range(KK if i < 2 else SYNC_TAPS):
                    o = (t // 3) * AR + t % 3
                    sync.dma_start(im2col[t * B * 2:(t + 1) * B * 2, n0:n1],
                                   attpad[:, o + n0:o + n1]).then_inc(im2col_ready[i], 16)
            sync.wait_ge(sig_used, NCH + CREDIT)
            sync.dma_start(px[SELK - 2:SELK, :, :], d["prow"].bitcast(bf16)).then_inc(px_ready, 16)

            def store_parts(q):
                sync.wait_ge(xparts_ready, 2 * (q + 1))
                for b in range(B):
                    sync.dma_start(scratch.rearrange("(b q c) f -> b c q f", b=B, q=NPART)
                                   [b, :, :, PIECES[q][0] * P128:PIECES[q][1] * P128],
                                   xparts[b * C:(b + 1) * C, :, PIECES[q][0] * P128:PIECES[q][1] * P128])\
                        .then_inc(xparts_stored, 16)

            def load_piece(b, q):
                f0, f1 = LOADS[q][0] * P128, LOADS[q][1] * P128
                rows = scratch.rearrange("(b r) f -> b r f", b=B)[ds(b, 1), :, f0:f1]\
                    .rearrange("b r f -> (b r) f")
                sync.dma_start(xs_sb[0:NPART * C, f0:f1], rows).then_inc(xs_loaded, 16)
                sync.dma_start(xs_sb[NPART * C:P128, f0:f1], rows[0:C, :]).then_inc(xs_loaded, 16)

            def regroup_offsets(q):
                n = CH_ROWS * W
                sync.wait_ge(px_ready, 16 * (1 + q * PX_DMAS))
                sync.wait_ge(tp_saved, q + 1 + CREDIT)
                for g in range(2):
                    for k in range(KK):
                        sync.dma_start(px[g * NXP:(g + 1) * NXP, k, q * n:(q + 1) * n],
                                       tpart[k * NXP:(k + 1) * NXP,
                                             g * HH * W + q * n:g * HH * W + (q + 1) * n])\
                            .then_inc(px_ready, 16)

            store_parts(0)
            for q in range(NQ - 2):
                store_parts(q + 1)
                regroup_offsets(q)
            sync.wait_ge(off_ready, HH + CREDIT)
            sync.wait_ge(xparts_stored, 16 * B * (NQ - 1))
            load_piece(0, 0)
            store_parts(NQ - 1)
            for q in range(1, NQ):
                if q < 3:
                    regroup_offsets(NQ - 3 + q)
                sync.wait_ge(xs_loaded, 32 * q)
                if q == NQ - 1:
                    sync.wait_ge(xparts_stored, 16 * B * NQ)
                load_piece(0, q)
            with sync.Fori(1, B) as b:
                for q in range(NQ):
                    sync.wait_ge(zrow_made, b * HH + ((q + 1) * CH_ROWS - HH + 2))
                    sync.sem_inc(load_turns, 1)
                    sync.wait_ge(xs_loaded, b * (32 * NQ) + 32 * q)
                    sync.sem_inc(load_turns, 1)
                    load_piece(b, q)
            for c in range(NCH):
                sync.wait_ge(res_ready, c + 1)
                sync.dma_start(out[:, c * BANK:(c + 1) * BANK], x_sb[:, c * BANK:(c + 1) * BANK])\
                    .then_inc(stored, 16)
            sync.wait_ge(stored, 16 * NCH)

        @block.gpsimd
        def _(pool):
            pool.memset(w0[:, :, :], 0.0).then_inc(w0_zeroed, 1)
            pool.memset(xpad[:, :, :], 0.0).then_inc(xpad_zeroed, 1)
            pool.memset(woff[:, :, :], 0.0).then_inc(zeroed, 1)
            pool.memset(wz[:, :, :], 0.0).then_inc(zeroed, 1)
            pool.memset(attpad, 0.0).then_inc(attpad_zeroed, 1)
            pool.memset(hx[:, :, :, :], 0.0).then_inc(hx_zeroed, 1)
            c0, c1, saved = MAP_PARTS[2]
            pool.wait_ge(att_saved, saved + CREDIT)
            n0, n1 = c0 * CH_ROWS * AR, min(c1 * CH_ROWS * AR, IMLEN - 2)
            for t in range(SYNC_TAPS, KK):
                o = (t // 3) * AR + t % 3
                pool.dma_start(im2col[t * B * 2:(t + 1) * B * 2, n0:n1],
                               attpad[:, o + n0:o + n1]).then_inc(im2col_rest, 16)
            def stage_row(slot, row):
                for dx in range(3):
                    pool.tensor_copy(stage[:, slot, dx, :].rearrange("p (g x) -> p g x", g=2),
                                     pair(row)[:, :, dx:dx + W]).then_inc(row_staged, 1)

            pool.wait_ge(norm2, 2)
            for row in (2, 3, 4):
                pool.wait_ge(off_ready, row - 2 + CREDIT)
                stage_row(row % 4, row + PAD_T)
            pool.wait_ge(norm2, 4)
            with pool.Fori(1, HH // 4) as iy:
                y = iy * 4
                for u in range(4):
                    pool.wait_ge(off_ready, y + (u - 1 + CREDIT))
                    pool.sem_inc(pool_turns, 1)
                    stage_row((u + 1) % 4, y + (u + 1 + PAD_T))

            far_row = pool.alloc_register("far_row")

            def far_stage(b, y, row, n):
                pool.wait_ge(far_zmade, n + CREDIT)
                pool.sem_inc(pool_turns, 1)
                for i in range(2):
                    for ky in range(3):
                        for g in range(2):
                            at = y + (g * HH + ky - 1 + PAD_T) + (row * -1 if i else row)
                            pool.reg_alu(far_row, at + FAR, FAR + PAD_T - 1, ALU.max)
                            pool.reg_alu(far_row, far_row, FAR + PAD_T + H, ALU.min)
                            pool.reg_alu(far_row, far_row, FAR, ALU.subtract)
                            r = pool.snap(far_row, min_val=PAD_T - 1, max_val=PAD_T + H)
                            copy = pool.tensor_copy(far_x[:, i, ky, g * W:(g + 1) * W],
                                                    xpad[:, ds(r, 1), 1:1 + W]
                                                    .rearrange("p a x -> p (a x)"))
                copy.then_inc(far_staged, 1)

            pool.wait_ge(reach_ready, 2)
            pool.wait_ge(px_ready, 16 * (1 + NQ * PX_DMAS))
            far_rows(pool, lambda b, y, n: None, far_stage)

        @block.tensor
        def _(pe):
            pe.wait_ge(norm1, 1)
            pe.wait_ge(w0_loaded, 16 * B)

            def conv_chunk(c, u):
                for t in range(KK):
                    rows = xpad[:, ds(c * CH_ROWS + (PAD_T - 1 + t // 3), CH_ROWS), t % 3:t % 3 + W]
                    mm = pe.matmul(ps[:, u * BANK:(u + 1) * BANK], w0[:, t, :], rows,
                                   start=t == 0, stop=t == KK - 1)
                mm.then_inc(conv_ready, 1)

            def att_chunk(c, u):
                pe.wait_ge(f_ready, c + (1 + CREDIT))
                pe.wait_ge(att_saved, c + (CREDIT - 1))
                pe.matmul(ps[0:B * 2, (2 + u) * BANK:(3 + u) * BANK], attw[:, :],
                          f_sb[:, ds(c * BANK, BANK)], start=True, stop=True).then_inc(att_ready, 1)

            def map_chunk(c, u):
                pe.wait_ge(sig_ready, c + (CREDIT - 1))
                rows = im2col[:, ds(c * (CH_ROWS * AR), CH_ROWS * AR)]\
                    .rearrange("p (r x) -> p r x", x=AR)[:, :, 0:W]
                pe.matmul(ps[:, (4 + u) * BANK:(5 + u) * BANK], mapw[:, :], rows,
                          start=True, stop=True).then_inc(map_ready, 1)

            conv_chunk(0, 0)
            pe.wait_ge(attw_ready, 1)
            with pe.Fori(0, NCH // 2 - 1) as ic:
                c = ic * 2
                for u in range(2):
                    if u == 0:
                        pe.wait_ge(norm1, ic + 2)
                    pe.wait_ge(f_ready, c + (u + CREDIT))
                    conv_chunk(c + (u + 1), 1 - u)
                    att_chunk(c + u, u)
            pe.wait_ge(mapw_ready, 1)
            pe.wait_ge(pos_loaded, 16)
            pe.wait_ge(im2col_ready[0], 16 * KK)
            for c in range(MAP_PARTS[0][0], MAP_PARTS[0][1]):
                map_chunk(c, c % 2)
            att_chunk(NCH - 2, 0)
            pe.wait_ge(norm1, NORM1)
            pe.wait_ge(f_ready, NCH - 2 + CREDIT)
            conv_chunk(NCH - 1, 1)
            att_chunk(NCH - 1, 1)
            def keep_clock(n):
                for _ in range(n):
                    pe.matmul(ps[:, 7 * BANK:8 * BANK], mapw[:, :],
                              im2col[:, 0:CH_ROWS * AR].rearrange("p (r x) -> p r x", x=AR)[:, :, 0:W],
                              start=True, stop=True)

            for i in (1, 2):
                if i == 2:
                    keep_clock(5)
                pe.wait_ge(im2col_ready[i], 16 * (KK if i < 2 else SYNC_TAPS))
                if i == 2:
                    pe.wait_ge(im2col_rest, 16 * (KK - SYNC_TAPS))
                for c in range(MAP_PARTS[i][0], MAP_PARTS[i][1]):
                    map_chunk(c, c % 2)

            pe.wait_ge(late_loaded, 16 * NLATE)

            def distance(b, y, bank=0):
                w = sel[:, ds(b, 1), :].rearrange("p a n -> p (a n)")
                first = BANK // W
                for k0, k1 in ((first, KK), (0, first)):
                    mm = pe.matmul(dist_ps(bank)[:, k0 * W:k1 * W], w,
                                   px[:, k0:k1, ds(y * W, W)], start=True, stop=True)
                mm.then_inc(dist_made, 1)

            def conv_quarter(q, between=None):
                for u in range(CH_ROWS):
                    if between and u == 4:
                        between()
                    rows = q * (3 * CH_ROWS) + u * 3
                    pe.wait_ge(off_saved, q * CH_ROWS + (u - 4 + CREDIT + 1))
                    for t in range(KK):
                        if t == 2 * KK // 3:
                            if isinstance(rows, int) and rows == 0:
                                pe.wait_ge(second_staged, 3)
                            else:
                                pe.wait_ge(row_staged, rows)
                        mm = pe.matmul(ps[:, (u % 4) * BANK:(u % 4) * BANK + NCOL],
                                       stage[:, (u + t // 3 - 1) % 4, t % 3, :],
                                       woff[:, t, :], start=t == 0, stop=t == KK - 1)
                    mm.then_inc(off_ready, 1)

            def parts_quarter(q):
                pe.wait_ge(parts_ready, q + 1)
                pe.wait_ge(tp_saved, q + CREDIT)
                for i in range(CH_ROWS):
                    mm = pe.transpose(tp_ps[:, i * P128:(i + 1) * P128],
                                      parts[:, ds(q * CH_ROWS + i, 1), :, :, :]
                                      .rearrange("p y k q b -> p (y k q b)"), identh[:, :])
                mm.then_inc(tp_ready, 1)

            keep_clock(4)
            pe.wait_ge(st_ready, 2 * NCH - 1)
            keep_clock(4)
            pe.wait_ge(first_staged, 6)
            conv_quarter(0)
            with pe.Fori(1, NQ - 1) as q:
                conv_quarter(q)
                parts_quarter(q - 1)

            pe.wait_ge(px_ready, 16 * (1 + PX_DMAS))
            distance(0, 0, 6)

            def second():
                pe.wait_ge(dist_ready, 2)
                distance(0, 1, 6)

            conv_quarter(NQ - 1, second)
            parts_quarter(NQ - 2)
            def keep_clock_short(n):
                for _ in range(n):
                    pe.matmul(ps[:, 5 * BANK:6 * BANK], identh[0:SELK, :], px[:, 0, 0:BANK],
                              start=True, stop=True)

            keep_clock_short(2)
            pe.wait_ge(reach_in, NQ)
            pe.wait_ge(dist_ready, 3)
            pe.transpose(ps[:, 6 * BANK:6 * BANK + P128], reach[:, :], identf[:, :]).then_inc(reach_t, 1)
            keep_clock_short(5)
            parts_quarter(NQ - 1)
            pe.wait_ge(reach_col, 1)
            pe.matmul(ps[0:1, 7 * BANK:7 * BANK + P128], reach_c[:, 1:2], identf[:, :],
                      start=True, stop=True).then_inc(reach_row, 1)

            pe.wait_ge(reach_read, 1)

            def z_row(n, u, bank=6):
                for i in range(2):
                    mm = pe.matmul(z_ps(u, bank), xs_sb[:, ds(n * P128, P128)], wzp[:, i, :],
                                   start=i == 0, stop=i == 1)
                return mm

            pe.wait_ge(wzp_ready, 4)
            keep_clock_short(3)
            with pe.Fori(0, B) as b:
                pe.wait_ge(xs_loaded, b * (32 * NQ) + 32)
                pe.wait_ge(zrow_saved, b * HH + CREDIT)
                for j in range(ZLEAD):
                    if j == 2:
                        pe.wait_ge(g_used, b * HH + (CREDIT - 1))
                    if j >= 4:
                        pe.wait_ge(lead_saved, b * ZLEAD + (j - 3))
                    z_row(j, j % 2, LEAD_BANKS[j]).then_inc(lead_made, 1)
                lead = pe.snap(b * ZLEAD + ZLEAD, min_val=ZLEAD, max_val=B * ZLEAD)
                loaded = pe.snap(b * (32 * NQ) + 32, min_val=32, max_val=32 * NQ * B)
                with pe.Fori(0, NQ) as q:
                    pe.wait_ge(xs_loaded, q * 32 + loaded)
                    pe.wait_ge(px_ready, ((q + 1) % NQ) * (16 * PX_DMAS) + 16 * (1 + PX_DMAS))
                    y = pe.snap(q * CH_ROWS, min_val=0, max_val=HH - CH_ROWS)
                    next_y = pe.snap((y + CH_ROWS) % HH, min_val=0, max_val=HH - CH_ROWS)
                    next_b = pe.snap(b + (y + CH_ROWS) // HH, min_val=0, max_val=B)
                    turn = [pe.snap(b * HH + y + (i + 3), min_val=3, max_val=NT + 3)
                            for i in range(CH_ROWS)]
                    for i in range(CH_ROWS):
                        u = i % 2
                        pe.wait_ge(dist_ready, turn[i])
                        if i + 2 < CH_ROWS:
                            distance(b, y + (i + 2))
                        else:
                            distance(next_b, next_y + (i + 2 - CH_ROWS))
                        if i == 0:
                            pe.wait_ge(lead_saved, lead)
                        pe.wait_ge(zrow_saved, turn[i])
                        z_row(y + (ZLEAD + i), u).then_inc(zrow_made, 1)
                        pe.wait_ge(hx_ready, turn[i])
                        pe.wait_ge(g_used, turn[i])
                        for h in range(2):
                            for j, k in enumerate(TAPS[h]):
                                mm = pe.matmul(g_ps(u, h)[:, j, :, :], hx[:, u, k, :],
                                               z_sb[:, ds(y + (i + k // 3), 3), k * C:(k + 1) * C],
                                               start=True, stop=True)
                        mm.then_inc(g_ready, 1)

            def far_tile(b, y, n):
                pe.wait_ge(dist_ready, n + (NT + 3))
                distance(b, y)

            def far_turn(b, y, row, n):
                pe.wait_ge(far_staged, n + 1)
                for i in range(2):
                    for ky in range(3):
                        s = slice(ky * 3 * C, (ky + 1) * 3 * C)
                        mm = pe.matmul(z_ps(i)[:, s], far_x[:, i, ky, :],
                                       wz[:, ds(b, 1), s], start=True, stop=True)
                mm.then_inc(far_zmade, 1)
                pe.wait_ge(far_zsaved, n + 1)
                pe.wait_ge(far_used, n + CREDIT)
                for h in range(2):
                    for j, k in enumerate(TAPS[h]):
                        mm = pe.matmul(far_ps[h][:, j, :, :], hx[:, 0, k, :], far_z[:, k, :, :],
                                       start=True, stop=True)
                mm.then_inc(far_made, 1)

            pe.wait_ge(acc_ready, NT)
            pe.wait_ge(zrow_saved, NT + CREDIT)
            pe.wait_ge(px_ready, 16 * (1 + NQ * PX_DMAS))
            far_rows(pe, far_tile, far_turn)

            pe.wait_ge(acc_final, 1)
            pe.wait_ge(dist_ready, NT + 3)
            for c in range(NCH):
                if c >= 4:
                    pe.wait_ge(outt_saved, c - 3)
                for i in range(4):
                    mm = pe.transpose(ps[:, (c % 4) * BANK + i * P128:(c % 4) * BANK + (i + 1) * P128],
                                      acc[:, 4 * c + i, :, :].rearrange("p b o -> p (b o)"), identf[:, :])
                mm.then_inc(outt_made, 1)
            pe.wait_ge(bst_ready, 1)
            pe.matmul(ps[:, 4 * BANK:4 * BANK + 1], avg4[:, :], col(MVB), start=True, stop=True)\
                .then_inc(bmean_ready, 1)
            pe.wait_ge(bvar_in, 1)
            pe.matmul(ps[:, 5 * BANK:5 * BANK + 1], avg4[:, :], col(SQ), start=True, stop=True)\
                .then_inc(bvar_ready, 1)

        @block.scalar
        def _(act):
            act.wait_ge(warm_in, 1)
            act.activation(warm[:, 1:2], warm[:, 0:1], ACT.Sqrt).then_inc(warmed, 1)
            act.dma_start(vec[:, :], d["vec"]).then_inc(params_loaded, 16)
            act.dma_start(attm[:, :], d["attm"]).then_inc(params_loaded, 16)
            act.dma_start(attp[:, :, :], d["attp"]).then_inc(map_loaded, 16)
            act.dma_start(attt[:, :, :], d["attt"]).then_inc(map_loaded, 16)
            act.dma_start(rowm[:, :], d["rowm"]).then_inc(map_loaded, 16)
            act.dma_start(blkm[:, :, :], d["blkm"]).then_inc(map_loaded, 16)
            act.dma_start(tile_code[:, :], d["tcode"]).then_inc(map_loaded, 16)

            def root(i, n=P128, w=1):
                act.wait_ge(root_in, i + 1)
                act.activation(small[0:n, ROOT_OUT:ROOT_OUT + w], small[0:n, ROOT_IN:ROOT_IN + w],
                               ACT.Sqrt).then_inc(root_done, 1)

            root(0)
            root(1)
            root(2, MAP_ROWS, 2)
            act.activation(warm[:, 2:3], warm[:, 0:1], ACT.Sigmoid).then_inc(warmed, 1)
            act.wait_ge(bn0_ready, 1)

            def save_branches(c, u):
                act.wait_ge(conv_ready, c + 1)
                act.activation(f_sb[:, ds(c * BANK, BANK)], ps[:, u * BANK:(u + 1) * BANK],
                               ACT.Identity, bias=col(BB), scale=col(BS)).then_inc(f_ready, 1)

            def sigmoid_map(c, u):
                act.wait_ge(map_ready, c + 1)
                act.wait_ge(sig_used, c + (CREDIT - 1))
                act.activation(sig[:, u, :], ps[:, (4 + u) * BANK:(5 + u) * BANK], ACT.Sigmoid)\
                    .then_inc(sig_ready, 1)

            with act.Fori(0, NCH // 2 - 1) as ic:
                for u in range(2):
                    save_branches(ic * 2 + u, u)
            save_branches(NCH - 2, 0)
            for c in range(MAP_PARTS[0][1]):
                sigmoid_map(c, c % 2)
            save_branches(NCH - 1, 1)
            for c in range(MAP_PARTS[0][1], NCH):
                sigmoid_map(c, c % 2)
            act.activation(warm[:, 3:4], warm[:, 0:1], ACT.Sqrt).then_inc(warmed, 1)
            root(3)
            act.activation(warm[:, 4:5], warm[:, 0:1], ACT.Sigmoid).then_inc(warmed, 1)
            act.wait_ge(norm2, 2)
            for dx in range(3):
                act.activation(stage[:, 1, dx, :].rearrange("p (g x) -> p g x", g=2),
                               pair(PAD_T + 1)[:, :, dx:dx + W], ACT.Copy).then_inc(second_staged, 1)
            act.wait_ge(rbias_ready, 3)

            def distance(u, bank=0):
                act.activation(dist[:, u, :], dist_ps(bank), ACT.Abs)\
                    .then_inc(dist_ready, 1)

            def weights(u):
                for g in range(2):
                    s = slice(g * W, (g + 1) * W)
                    relu = act.activation(hx[s, u, :, s],
                                          dist[s, u, :].rearrange("p (k x) -> p k x", k=KK),
                                          ACT.Relu, bias=rbias[s, 0:1], scale=-1.0)
                relu.then_inc(hx_ready, 1)

            def offsets(q):
                rows = ds(q * CH_ROWS, CH_ROWS)
                act.wait_ge(off_saved, q * CH_ROWS + (CH_ROWS + CREDIT))
                act.activation(mod_v[:, rows], mod_v[:, rows], ACT.Sigmoid).then_inc(mod_ready, 1)
                for r in range(3):
                    act.activation(per_tile(hy[:, r, :])[:, rows], oy_v[:, rows], ACT.Abs,
                                   bias=rbias[:, r:r + 1]).then_inc(hya_ready, 1)

            def save_parts(q):
                rows = ds(q * CH_ROWS, CH_ROWS)
                act.wait_ge(tp_ready, q + 1)
                dst = tpart[0:NPART * B * KK, :].rearrange("p (g y x) -> p g y x", g=2, x=W)
                act.activation(dst[:, :, rows, :], tp_ps.rearrange("p (y g x) -> p g y x", y=CH_ROWS, g=2),
                               ACT.Copy).then_inc(tp_saved, 1)

            offsets(0)
            with act.Fori(1, NQ - 1) as q:
                offsets(q)
                save_parts(q - 1)
            act.wait_ge(hx_zeroed, 1)
            act.wait_ge(dist_made, 1)
            distance(0, 6)
            act.wait_ge(dist_ready, 2)
            weights(0)
            act.wait_ge(dist_made, 2)
            distance(1, 6)
            save_parts(NQ - 2)
            offsets(NQ - 1)
            save_parts(NQ - 1)
            with act.Fori(0, B) as b:
                act.wait_ge(xparts_stored, 16 * B * (NQ - 1))
                for j in range(ZLEAD):
                    act.wait_ge(lead_made, b * ZLEAD + (j + 1))
                    act.activation(z_sb[:, j, :], z_ps(j % 2, LEAD_BANKS[j]), ACT.Copy).then_inc(lead_saved, 1)
                with act.Fori(0, NQ) as q:
                    act.wait_ge(xparts_stored, (q + (NQ - 1)) // NQ * (16 * B) + 16 * B * (NQ - 1))
                    y = act.snap(q * CH_ROWS, min_val=0, max_val=HH - CH_ROWS)
                    turn = [act.snap(b * HH + y + (i + 3), min_val=3, max_val=NT + 3)
                            for i in range(CH_ROWS)]
                    for i in range(CH_ROWS):
                        u = i % 2
                        act.wait_ge(hx_ready, turn[i])
                        act.wait_ge(dist_made, turn[i])
                        distance(u)
                        act.wait_ge(dist_ready, turn[i])
                        act.wait_ge(g_ready, turn[i])
                        weights(1 - u)
                        act.wait_ge(zrow_made, turn[i])
                        act.activation(z_sb[:, ds(y + (ZLEAD + i), 1), :], z_ps(u), ACT.Copy)\
                            .then_inc(zrow_saved, 1)

            def far_tile(b, y, n):
                act.wait_ge(dist_made, n + (NT + 3))
                act.wait_ge(hx_ready, n + (NT + 3))
                act.activation(dist[:, 0, :], dist_ps(0), ACT.Abs).then_inc(dist_ready, 1)
                act.wait_ge(dist_ready, n + (NT + 4))
                for g in range(2):
                    s = slice(g * W, (g + 1) * W)
                    relu = act.activation(hx[s, 0, :, s],
                                          dist[s, 0, :].rearrange("p (k x) -> p k x", k=KK),
                                          ACT.Relu, bias=rbias[s, 0:1], scale=-1.0)
                relu.then_inc(hx_ready, 1)

            def far_turn(b, y, row, n):
                act.wait_ge(far_zmade, n + (1 + CREDIT))
                for i in range(2):
                    save = act.activation(far_z[:, :, i, :],
                                          z_ps(i).rearrange("p (k o) -> p k o", k=KK), ACT.Copy)
                save.then_inc(far_zsaved, 1)

            act.wait_ge(reach_ready, 2)
            far_rows(act, far_tile, far_turn)

            act.activation(warm[:, 5:6], warm[:, 0:1], ACT.Sqrt).then_inc(warmed, 1)
            for c in range(NCH):
                act.wait_ge(outt_made, c + 1)
                dst = out_t.rearrange("p (g y x) -> p g y x", g=2, x=W)
                act.activation(dst[:, :, 4 * c:4 * c + 4, :],
                               ps[:, (c % 4) * BANK:(c % 4 + 1) * BANK]
                               .rearrange("p (y g x) -> p g y x", y=4, g=2),
                               ACT.Identity, bias=vec[:, V_DBIAS:V_DBIAS + 1]).then_inc(outt_saved, 1)
            root(4)
            act.wait_ge(bnc_ready, 1)
            for c in range(NCH):
                act.activation(out_t[:, c * BANK:(c + 1) * BANK], out_t[:, c * BANK:(c + 1) * BANK],
                               ACT.Relu, bias=col(SH), scale=col(SC)).then_inc(relu_ready, 1)

        @block.vector
        def _(vector):
            links = 0
            roots = 0

            def chain(ins):
                nonlocal links
                links += 1
                ins.then_inc(vchain, 1)
                vector.wait_ge(vchain, links)

            def rstd(dst, var, eps):
                nonlocal roots
                n, w = dst.shape
                v, r, t = (small[0:n, i:i + w] for i in (ROOT_IN, ROOT_OUT, ROOT_TMP))
                vector.tensor_scalar(v, var, eps, None, ALU.add).then_inc(root_in, 1)
                roots += 1
                vector.wait_ge(root_done, roots)
                chain(vector.reciprocal(dst, r))
                chain(vector.tensor_tensor(t, dst, dst, ALU.mult))
                chain(vector.scalar_tensor_tensor(t, t, -0.5, v, ALU.mult, ALU.mult))
                chain(vector.scalar_tensor_tensor(dst, t, 1.5, dst, ALU.add, ALU.mult))

            vector.memset(warm[:, :], 1.0).then_inc(warm_in, 1)
            for s_ in (far_zmade, far_used, f_ready, att_saved, sig_ready, sig_used, off_ready, off_saved, tp_saved,
                       zrow_saved, g_used):
                vector.sem_inc(s_, CREDIT)
            for s_, n in ((dist_ready, 1), (hx_ready, 2), (zrow_made, 2), (g_ready, 3)):
                vector.sem_inc(s_, n)
            for r in range(3):
                vector.memset(rbias[:, r:r + 1], 1.0 - r).then_inc(rbias_ready, 1)
            for c in range(NCH):
                if c in X_ENDS:
                    vector.wait_ge(x_loaded[X_ENDS.index(c)], 16)
                vector.bn_stats(stats[:, c, :], x_sb[:, c * BANK:(c + 1) * BANK]).then_inc(st_ready, 1)
            vector.wait_ge(st_ready, NCH)
            chain(vector.bn_aggr(small[:, MV:MV + 2], stats[:, :, :]))
            rstd(col(RSTD), col(MV + 1), GN_EPS)
            vector.wait_ge(xpad_zeroed, 1)
            inner = xpad[:, PAD_T:PAD_T + H, 1:1 + W]
            x3 = x_sb[:, :].rearrange("p (y x) -> p y x", y=H)
            ends = [0] + [min((2 * i + 1) * CH_ROWS + 1, H) for i in range(NORM1)]
            for r0, r1 in zip(ends[:-1], ends[1:]):
                vector.tensor_scalar(inner[:, r0:r1, :], x3[:, r0:r1, :], col(MV), col(RSTD),
                                     ALU.subtract, ALU.mult).then_inc(norm1, 1)

            vector.wait_ge(params_loaded, 32)
            p_ = lambda i: vec[:, i:i + 1]
            rstd(col(BS), p_(V_VAR), BR_EPS)
            chain(vector.tensor_tensor(col(BS), col(BS), p_(V_GAMMA), ALU.mult))
            chain(vector.tensor_tensor(col(BB), p_(V_CB), p_(V_MEAN), ALU.subtract))
            vector.scalar_tensor_tensor(col(BB), col(BB), col(BS), p_(V_BETA), ALU.mult, ALU.add)\
                .then_inc(bn0_ready, 1)
            vector.tensor_scalar(attw[:, :], attm[:, :], p_(V_ATTW), None, ALU.mult)\
                .then_inc(attw_ready, 1)
            vector.wait_ge(map_loaded, 80)
            R = MAP_ROWS
            a_ = lambda i: attp[:, i, :]
            t0, t1 = small[0:R, T0:T0 + 2], small[0:R, T1:T1 + 2]
            s_att, u_ = small[0:R, 21:23], small[0:R, 23:25]
            M_ATT, M_GH, M_GW, M_PR, M_ONE = (rowm[:, i:i + 1] for i in range(5))
            rstd(s_att, a_(A_VAR), ATT_EPS)
            chain(vector.tensor_tensor(s_att, s_att, a_(A_GAMMA), ALU.mult))
            chain(vector.tensor_tensor(t0, a_(A_B), a_(A_MEAN), ALU.subtract))
            chain(vector.tensor_scalar(u_, t0, M_ONE, M_ATT, ALU.mult, ALU.add))
            chain(vector.scalar_tensor_tensor(u_, a_(A_WGH), M_GH, u_, ALU.mult, ALU.add))
            chain(vector.scalar_tensor_tensor(u_, a_(A_WGW), M_GW, u_, ALU.mult, ALU.add))
            chain(vector.tensor_tensor(u_, u_, s_att, ALU.mult))
            chain(vector.scalar_tensor_tensor(u_, a_(A_BETA), M_ONE, u_, ALU.mult, ALU.add))
            chain(vector.tensor_tensor(u_, u_, attt[:, 0, :], ALU.mult))
            chain(vector.tensor_scalar(t1, attt[:, 1, :], M_GH, None, ALU.mult))
            chain(vector.scalar_tensor_tensor(t1, attt[:, 1, :], M_GW, t1, ALU.mult, ALU.add))
            chain(vector.scalar_tensor_tensor(t1, attt[:, 1, :], M_PR, t1, ALU.mult, ALU.add))
            chain(vector.tensor_tensor(u_, u_, t1, ALU.add))
            chain(vector.tensor_scalar(mapw[:, :], blkm[:, 0, :], small[0:R, 23:24], None, ALU.mult))
            vector.scalar_tensor_tensor(mapw[:, :], blkm[:, 1, :], small[0:R, 24:25], mapw[:, :],
                                        ALU.mult, ALU.add).then_inc(mapw_ready, 1)

            vector.wait_ge(wz_loaded, 16 * 4)
            wzq = [wz_parts[:, i, :] for i in range(3)]
            chain(vector.tensor_copy(wzq[0], wz_rep))
            chain(vector.tensor_tensor(wz_rest, wz_rep, wzq[0], ALU.subtract))
            chain(vector.tensor_copy(wzq[1], wz_rest))
            chain(vector.tensor_tensor(wzq[2], wz_rest, wzq[1], ALU.subtract))
            chain(vector.memset(wzp[:, 1, :], 0.0))
            for i, group, part in ((0, slice(0, 3 * C), 0), (0, slice(3 * C, 4 * C), 1),
                                   (1, slice(0, C), 2), (1, slice(C, 2 * C), 1)):
                vector.tensor_copy(wzp[group, i, :], wz_parts[group, part, :]).then_inc(wzp_ready, 1)

            vector.wait_ge(attpad_zeroed, 1)
            att3 = attpad.rearrange("p (r x) -> p r x", x=AR)

            def save_att(c, u):
                vector.wait_ge(att_ready, c + 1)
                vector.tensor_copy(att3[:, ds(c * CH_ROWS + 1, CH_ROWS), 1:1 + W],
                                   ps[0:B * 2, (2 + u) * BANK:(3 + u) * BANK]
                                   .rearrange("p (r x) -> p r x", x=W)).then_inc(att_saved, 1)

            def add_branches(c):
                xs = [x_sb[:, (c + u) * BANK:(c + u + 1) * BANK] for u in range(2)]
                for u in range(2):
                    vector.wait_ge(sig_ready, c + u + 1 + CREDIT)
                    vector.scalar_tensor_tensor(prod[:, u, 0:BANK], sig[:, u, :], p_(V_SCALE),
                                                f_sb[:, (c + u) * BANK:(c + u + 1) * BANK],
                                                ALU.mult, ALU.mult).then_inc(sig_used, 1)
                for u in range(2):
                    vector.wait_ge(sig_used, c + u + 1 + CREDIT)
                    vector.tensor_tensor(xs[u], prod[:, u, 0:BANK], xs[u], ALU.add).then_inc(x1_ready, 1)
                for u in range(2):
                    vector.wait_ge(x1_ready, c + u + 1)
                    vector.bn_stats(stats[:, c + u, :], xs[u]).then_inc(st_ready, 1)

            with vector.Fori(0, NCH // 2 - 1) as ic:
                for u in range(2):
                    save_att(ic * 2 + u, u)
            add_branches(0)
            save_att(NCH - 2, 0)
            add_branches(2)
            save_att(NCH - 1, 1)
            for c in range(MAP_PARTS[0][1], NCH, 2):
                add_branches(c)
            vector.wait_ge(st_ready, 2 * NCH)
            chain(vector.bn_aggr(small[:, MV2:MV2 + 2], stats[:, :, :]))
            rstd(col(RSTD2), col(MV2 + 1), GN_EPS)
            pieces2 = ((0, FIRST), (HH - 1, HH + FIRST), (FIRST, HH - 1), (HH + FIRST, H))
            for i, (r0, r1) in enumerate(pieces2):
                vector.tensor_scalar(inner[:, r0:r1, :], x3[:, r0:r1, :], col(MV2),
                                     col(RSTD2), ALU.subtract, ALU.mult).then_inc(norm2, 1)
                if i == 1:
                    vector.wait_ge(norm2, 2)
                    for slot, row in ((3, PAD_T - 1), (0, PAD_T)):
                        for dx in range(3):
                            vector.tensor_copy(stage[:, slot, dx, :].rearrange("p (g x) -> p g x", g=2),
                                               pair(row)[:, :, dx:dx + W]).then_inc(first_staged, 1)

            vector.wait_ge(late_loaded, 16 * NLATE)
            links_q = 6

            def link(ins, q, n):
                ins.then_inc(quarter_link, 1)
                vector.wait_ge(quarter_link, q * links_q + (n + 1))

            def split_rows(q, step):
                n = PIECES[q][1] - PIECES[q][0] if isinstance(q, int) else ZPIECE
                src = [xpad[:, ds(q * ZPIECE + g * HH, n), 1:1 + W] for g in range(2)]
                rest = xrest[:, 0:n * P128].rearrange("p (n g x) -> p g n x", g=2, x=W)
                dst = [xparts[:, i, ds(q * (ZPIECE * P128), n * P128)]
                       .rearrange("p (n g x) -> p g n x", g=2, x=W) for i in range(NPART)]
                if step > 0:
                    vector.wait_ge(split, q * 6 + 2 * step)
                for g in range(2):
                    if step == 0:
                        vector.tensor_copy(dst[0][:, g], src[g]).then_inc(split, 1)
                    elif step == 1:
                        vector.tensor_tensor(rest[:, g], src[g], dst[0][:, g], ALU.subtract).then_inc(split, 1)
                    elif step == 2:
                        vector.tensor_copy(dst[1][:, g], rest[:, g]).then_inc(split, 1)
                    else:
                        vector.tensor_tensor(dst[2][:, g], rest[:, g], dst[1][:, g],
                                             ALU.subtract).then_inc(xparts_ready, 1)

            def offsets(q):
                y = q * CH_ROWS
                for u in range(CH_ROWS):
                    vector.wait_ge(off_ready, y + (u + 1 + CREDIT))
                    vector.tensor_tensor(offs[:, ds(y + u, 1), :],
                                         ps[:, (u % 4) * BANK:(u % 4) * BANK + NCOL],
                                         offb[:, :], ALU.add).then_inc(off_saved, 1)
                    if u % 2 == 0:
                        split_rows(q, u // 2)
                vector.wait_ge(off_saved, y + (CH_ROWS + CREDIT))
                rows = ds(y, CH_ROWS)
                vector.tensor_reduce(reach[:, :].rearrange("p (y b) -> p y b", b=B)[:, rows],
                                     oy_v[:, rows], AX.X, ALU.max,
                                     apply_absolute_value=True).then_inc(reach_in, 1)
                rest = hyt[:, 0:CH_ROWS * B * KK].rearrange("p (y b k) -> p y b k", y=CH_ROWS, b=B)
                part = [parts[:, rows, :, i, :].rearrange("p y k b -> p y b k") for i in range(NPART)]
                link(vector.tensor_copy(part[0], ox_v[:, rows]), q, 0)
                link(vector.tensor_tensor(rest, ox_v[:, rows], part[0], ALU.subtract), q, 1)
                link(vector.tensor_copy(part[1], rest), q, 2)
                vector.tensor_tensor(part[2], rest, part[1], ALU.subtract).then_inc(parts_ready, 1)

            def vertical_weights(q):
                rows = ds(q * CH_ROWS, CH_ROWS)
                vector.wait_ge(mod_ready, q + 1)
                for r in range(3):
                    hyr = per_tile(hy[:, r, :])[:, rows]
                    vector.wait_ge(hya_ready, q * 3 + (r + 1))
                    link(vector.tensor_scalar(hyr, hyr, -1.0, 0.0, ALU.add, ALU.min), q, 3 + r)
                    vector.scalar_tensor_tensor(hyr, hyr, -2.0, mod_v[:, rows], ALU.mult, ALU.mult)\
                        .then_inc(hy_ready, 1)

            vector.wait_ge(norm2, 4)
            with vector.Fori(0, NQ - 1) as q:
                offsets(q)
                vertical_weights(q)
            offsets(NQ - 1)
            vector.wait_ge(reach_t, 1)
            chain(vector.tensor_reduce(reach_c[:, 0:1], ps[:, 6 * BANK:6 * BANK + P128], AX.X, ALU.max))
            chain(vector.tensor_scalar(reach_c[:, 1:2], reach_c[:, 0:1], float(FAR - 1), None, ALU.min))
            vector.scalar_tensor_tensor(reach_c[:, 1:2], reach_c[:, 0:1], 1.0, reach_c[:, 1:2],
                                        ALU.is_ge, ALU.mult).then_inc(reach_col, 1)
            vector.wait_ge(reach_row, 1)
            vector.tensor_copy(reach_i[:, :], ps[0:1, 7 * BANK:7 * BANK + P128]).then_inc(reach_read, 1)
            vertical_weights(NQ - 1)
            vector.wait_ge(reach_read, 1)
            chain(vector.tensor_copy(far_code[:, 1, 0:NT], reach_i[:, :]))
            chain(vector.memset(far_code[:, 0, :], float(FAR1 * NT)))
            chain(vector.tensor_tensor(tile_code[:, :], tile_code[:, :], far_code[:, 1, 0:NT], ALU.add))
            chain(vector.scalar_tensor_tensor(far_code[:, 0, 0:NT], far_code[:, 1, 0:NT], 1.0,
                                              tile_code[:, :], ALU.min, ALU.mult))
            chain(vector.tensor_scalar(far_code[:, 0, 0:NT], far_code[:, 0, 0:NT], float(FAR1 * NT),
                                       None, ALU.add))
            chain(vector.memset(far_code[:, 1, NT:2 * NT], float(FAR1 * NT)))
            for i in range(7):
                a_, b_ = far_code[:, i % 2, :], far_code[:, 1 - i % 2, :]
                chain(vector.tensor_tensor(b_[:, 0:NT], a_[:, 0:NT], a_[:, 1 << i:NT + (1 << i)], ALU.min))
            vector.tensor_copy(next_far[:, :], far_code[:, 1, 0:NT + 1]).then_inc(reach_ready, 2)
            vector.wait_ge(hy_ready, NQ * 3)
            with vector.Fori(0, B) as b:
                with vector.Fori(0, HH // 2) as iy:
                    y = iy * 2
                    for u in range(2):
                        t = b * HH + y + u
                        wv = hy[:, :, ds(y * (B * KK) + b * KK + u * (B * KK), KK)]\
                            .rearrange("p r k -> p k r").unsqueeze(3).to_broadcast([P128, KK, 3, C])
                        vector.wait_ge(g_ready, b * HH + y + (u + 1 + 3))
                        pv = prod[:, u, :].rearrange("p (k r o) -> p k r o", k=KK, r=3)
                        for h in range(2):
                            k0, k1 = TAPS[h][0], TAPS[h][-1] + 1
                            mul = vector.tensor_tensor(pv[:, k0:k1], g_ps(u, h), wv[:, k0:k1], ALU.mult)
                        mul.then_inc(g_used, 1)
                        vector.wait_ge(g_used, b * HH + y + (u + 1 + CREDIT))
                        vector.tensor_reduce(acc[:, ds(y + u, 1), ds(b, 1), :],
                                             prod[:, u, :].rearrange("p (n o) -> p o n", o=C),
                                             AX.X, ALU.add).then_inc(acc_ready, 1)

            def far_tile(b, y, n):
                vector.memset(far_r[:, :], 1.0).then_inc(far_turns, 1)

            def far_turn(b, y, row, n):
                oy = offs[:, ds(y, 1), ds(b * NOFF, KK)].rearrange("p a k -> p (a k)")
                mod = offs[:, ds(y, 1), ds(b * NOFF + 2 * KK, KK)].rearrange("p a k -> p (a k)")
                vector.drain()
                vector.tensor_scalar(far_r[:, :], far_r[:, :], 1.0, None, ALU.add)
                vector.drain()
                for i in range(2):
                    vector.tensor_scalar(far_w[:, :, i], oy, far_r[:, :], 2.0,
                                         ALU.add if i else ALU.subtract, ALU.mult)
                vector.drain()
                vector.tensor_scalar(far_u[:, :, :], far_w[:, :, :], -1.0, -2.0, ALU.mult, ALU.add)
                vector.drain()
                vector.scalar_tensor_tensor(far_w[:, :, :], far_w[:, :, :], -2.0, far_u[:, :, :],
                                            ALU.add, ALU.max)
                vector.drain()
                vector.scalar_tensor_tensor(far_w[:, :, :], far_w[:, :, :], 0.0,
                                            mod.unsqueeze(2).to_broadcast([P128, KK, 2]),
                                            ALU.min, ALU.mult)
                vector.drain()
                vector.wait_ge(far_made, n + 1)
                for h in range(2):
                    k0, k1 = TAPS[h][0], TAPS[h][-1] + 1
                    mul = vector.tensor_tensor(far_p[:, k0:k1], far_ps[h],
                                               far_w[:, k0:k1, :].unsqueeze(3)
                                               .to_broadcast([P128, k1 - k0, 2, C]), ALU.mult)
                mul.then_inc(far_used, 1)
                vector.drain()
                vector.tensor_reduce(far_s[:, :], far_p.rearrange("p k i o -> p o (k i)"),
                                     AX.X, ALU.add)
                vector.drain()
                here = acc[:, ds(y, 1), ds(b, 1), :].rearrange("p a c o -> p (a c o)")
                vector.tensor_tensor(here, here, far_s[:, :], ALU.subtract)
                vector.drain()

            vector.wait_ge(reach_ready, 2)
            vector.wait_ge(acc_ready, NT)
            far_rows(vector, far_tile, far_turn)
            vector.drain().then_inc(acc_final, 1)

            ot = out_t.rearrange("p (g y x) -> p g y x", g=2, x=W)
            for c in range(NCH):
                vector.wait_ge(outt_saved, c + 1)
                for g in range(2):
                    vector.bn_stats(bstats[:, 2 * c + g, :],
                                    ot[:, g, 4 * c:4 * c + 4, :].rearrange("p y x -> p (y x)"))\
                        .then_inc(st_ready, 1)
            vector.wait_ge(st_ready, 4 * NCH)
            chain(vector.bn_aggr(small[:, MVB:MVB + 2], bstats[:, :, :]))
            vector.tensor_copy(col(62), col(MVB)).then_inc(bst_ready, 1)
            vector.wait_ge(bmean_ready, 1)
            chain(vector.tensor_copy(col(MEANB), ps[:, 4 * BANK:4 * BANK + 1]))
            chain(vector.tensor_tensor(col(DB), col(MVB), col(MEANB), ALU.subtract))
            vector.scalar_tensor_tensor(col(SQ), col(DB), col(DB), col(MVB + 1), ALU.mult, ALU.add)\
                .then_inc(bvar_in, 1)
            vector.wait_ge(bvar_ready, 1)
            rstd(col(SC), ps[:, 5 * BANK:5 * BANK + 1], BN_EPS)
            chain(vector.tensor_tensor(col(SC), col(SC), p_(V_DGAMMA), ALU.mult))
            chain(vector.tensor_tensor(col(T0), col(MEANB), col(SC), ALU.mult))
            vector.tensor_tensor(col(SH), p_(V_DBETA), col(T0), ALU.subtract).then_inc(bnc_ready, 1)
            for c in range(NCH):
                s = slice(c * BANK, (c + 1) * BANK)
                vector.wait_ge(relu_ready, c + 1)
                vector.tensor_tensor(x_sb[:, s], x_sb[:, s], out_t[:, s], ALU.add)\
                    .then_inc(res_ready, 1)



def _lay_out(i):
    a = {k: np.asarray(v) for k, v in i.items()}
    L0 = lambda n: a["L0_conv_" + n]
    L1 = lambda n: a["L1_conv_" + n]
    f = np.float32

    def bf(v):
        return (np.ascontiguousarray(v, f).view(np.uint32) >> 16).astype(np.uint16)

    d = {"x": a["x"].reshape(P128, NPIX)}
    taps = lambda w: np.ascontiguousarray(w.reshape(w.shape[0], w.shape[1], KK))
    both = lambda n: np.concatenate([L0(n.replace("?", "a")), L0(n.replace("?", "b"))])
    d["w0"] = taps(both("conv_?_w")).transpose(1, 2, 0)
    cols = [both("conv_?_b"), both("bn_?_gamma"), both("bn_?_beta"), both("bn_?_mean"),
            both("bn_?_var"),
            np.concatenate([L0("att_a_w")[0, :BR, 0, 0], L0("att_b_w")[0, :BR, 0, 0]]),
            np.concatenate([np.broadcast_to(L0("scale1"), (BR,)), np.broadcast_to(L0("scale2"), (BR,))]),
            L1("bias"), L1("gamma"), L1("beta")]
    d["vec"] = np.tile(np.stack(cols, 1), (B, 1))
    ow, ob = L1("offset_w"), L1("offset_b")
    d["woff"] = taps(np.concatenate([ow[0::2], ow[1::2], L1("mod_w")])).transpose(1, 2, 0)
    d["offb"] = np.tile(np.concatenate([ob[0::2], ob[1::2], L1("mod_b")]), (P128, B))
    d["wz"] = taps(L1("weight")).transpose(1, 2, 0).reshape(C, KW)
    per = [[L0(f"att_{s}_w")[0, BR, 0, 0], L0(f"att_{s}_w")[0, BR + 1, 0, 0], L0(f"att_{s}_b")[0],
            L0(f"att_bn_{s}_gamma")[0], L0(f"att_bn_{s}_beta")[0], L0(f"att_bn_{s}_mean")[0],
            L0(f"att_bn_{s}_var")[0]] for s in "ab"]
    d["attp"] = np.tile(np.array(per, f).T[None], (MAP_ROWS, 1, 1))
    tap = np.concatenate([np.repeat(np.arange(KK), B * 2), np.repeat(np.arange(KK), 4)])
    chan = np.concatenate([np.zeros(ATT_ROWS, int), np.tile([1, 2, 3, 0], KK)])
    attn = np.stack([taps(L0("attn_a_w"))[0], taps(L0("attn_b_w"))[0]])
    d["attt"] = np.stack([attn[:, 0, tap], attn[:, chan, tap]]).transpose(2, 0, 1)
    kind = np.concatenate([np.zeros(ATT_ROWS, int), np.tile([1, 2, 3, 4], KK)])
    d["rowm"] = (kind[:, None] == np.arange(5)).astype(f)
    p = np.arange(P128)
    pb, pbr = p // C, (p % C) // BR
    rb = np.concatenate([np.tile(np.repeat(np.arange(B), 2), KK), np.full(POS_ROWS, -1)])
    rbr = np.concatenate([np.tile([0, 1], KK * B), np.full(POS_ROWS, -1)])
    m = np.stack([(pbr == s)[None] & ((rb[:, None] == -1) | ((rb[:, None] == pb) & (rbr[:, None] == s)))
                  for s in range(2)], 1)
    d["blkm"] = m.astype(f)
    q = np.arange(B * 2)
    d["attm"] = ((q[None] // 2 == pb[:, None]) & (q[None] % 2 == pbr[:, None])).astype(f)
    gh = np.abs(np.arange(H, dtype=f) - H // 2 + f(0.5)) / f(H // 2)
    gw = np.abs(np.arange(W, dtype=f) - W // 2 + f(0.5)) / f(W // 2)
    GHt, GWt = np.broadcast_to(gh[:, None], (H, W)), np.broadcast_to(gw[None], (H, W))
    pr = np.sqrt(GHt ** 2 + GWt ** 2)
    k = f(2.0) / (pr.max() - pr.min())
    pr = k * pr + (f(1.0) - pr.max() * k)
    pos = np.zeros((4, AR, AR), f)
    pos[:, 1:1 + H, 1:1 + W] = np.stack([GHt, GWt, pr, np.ones((H, W), f)])
    flat = np.concatenate([pos.reshape(4, AR * AR), np.zeros((4, 2 * AR), f)], 1)
    d["pos"] = np.concatenate([flat[:, (t // 3) * AR + t % 3:][:, :IMLEN] for t in range(KK)])
    d["avg4"] = ((p[:, None] % C) == (p[None] % C)).astype(f) / f(B)
    d["tcode"] = (128 * (np.arange(NT, dtype=f) - NT))[None]
    d["identf"] = np.eye(P128, dtype=f)
    d["identh"] = bf(np.eye(P128))
    sel = np.zeros((SELK, B + 1, P128), f)
    for b in range(B):
        for part in range(NPART):
            for g in range(2):
                sel[g * NXP + part * B + b, b, g * W:(g + 1) * W] = 1
        sel[SELK - 2, b] = 1
        sel[SELK - 1, b] = -(p % W)
    d["sel"] = bf(sel)
    xk = np.arange(W)[None] + (np.arange(KK) % 3 - 1)[:, None]
    prow = np.ones((2, KK, HH, W), f)
    prow[0] = xk[:, None, :]
    d["prow"] = bf(prow.reshape(2, KK, HH * W))
    return {n: np.ascontiguousarray(v) for n, v in d.items()}


def kernel(**inputs):
    import concourse.bacc as bacc
    from concourse.bass_utils import run_bass_kernel_spmd as run

    data = _lay_out(inputs)
    nc = bacc.Bacc("TRN2", target_bir_lowering=False, num_devices=1)
    arrays, aps = {}, {}
    for name, v in data.items():
        arrays[f"in_{name}"] = v
        aps[name] = nc.dram_tensor(f"in_{name}", v.shape, mybir.dt.from_np(v.dtype),
                                   kind="ExternalInput").ap()
    out = nc.dram_tensor("out", (P128, NPIX), mybir.dt.float32, kind="ExternalOutput").ap()
    scratch = nc.dram_tensor("scratch", (B * NPART * C, ZSLOTS * P128), mybir.dt.bfloat16).ap()
    conv_deform_kernel(nc, aps, scratch, out)
    r = run(nc, [arrays], core_ids=[0])
    return r.results[0]["out"].reshape(B, C, H, W)
```
